# Optimizing a Trainium2 kernel written in Bass

```python
import numpy as np
import jax
import jax.numpy as jnp

def _softmax(x, axis=-1):
    return jax.nn.softmax(x, axis=axis)

def _gelu(x):
    return jax.nn.gelu(x, approximate=True)

def _silu(x):
    return jax.nn.silu(x)

def _sigmoid(x):
    return jax.nn.sigmoid(x)

def _layernorm(x, axis=-1, eps=1e-05):
    m = jnp.mean(x, axis=axis, keepdims=True)
    v = jnp.var(x, axis=axis, keepdims=True)
    return (x - m) / jnp.sqrt(v + eps)

def _scatter_add(tgt, idx, src, axis=0):
    return tgt.at[idx].add(src)

def _segment_sum(src, seg, n):
    return jax.ops.segment_sum(src, seg, n)
kernel_name = 'mk_gnn_resnorm_d4_gnn_r8_50d453'

def setup_inputs(seed: int=0):
    np.random.seed(seed)
    _w = jnp.asarray

    def _rec_inputs():
        import jax
        import jax.numpy as jnp
        _gk = jax.random.key(seed)
        x = -0.000202 + 1 * jax.random.normal(jax.random.fold_in(_gk, 1), (6250, 128), jnp.float32)
        _s = jax.random.randint(jax.random.fold_in(_gk, 2), (100000,), 0, 6250, jnp.int32)
        _d = jax.random.randint(jax.random.fold_in(_gk, 3), (100000,), 0, 6250, jnp.int32)
        _loop = jnp.arange(6250, dtype=jnp.int32)
        src = jnp.concatenate([_s, _d, _loop])
        dst = jnp.concatenate([_d, _s, _loop])
        _o = jnp.argsort(dst, stable=True)
        src = src[_o]
        dst = dst[_o]
        edge_attr_128 = -4.21973e-05 + 0.999841 * jax.random.normal(jax.random.fold_in(_gk, 12), (206250, 128), jnp.float32)
        edge_type_8 = jax.random.randint(jax.random.fold_in(_gk, 14), (206250,), 0, 8, jnp.int32)
        return (x, src, dst, edge_attr_128, edge_type_8)
    x, src, dst, edge_attr_128, edge_type_8 = _rec_inputs()

    def _L0_gnn_setup():
        import jax, jax.numpy as jnp
        import numpy as np
        N = 6250
        E = 100000
        D = 128
        R = 8
        B = 4
        L = 2
        BN_EPS = 0.001

        def _edge_norm(etype, dst, dtype):
            node_norm = jnp.zeros((N,), dtype=dtype)
            for r in range(R):
                mask = (etype == r).astype(dtype)
                cnt = jax.ops.segment_sum(mask, dst, num_segments=N)
                node_norm = jnp.where(cnt > 0, 1.0 / jnp.maximum(cnt, 1.0), node_norm)
            return node_norm[dst][:, None]
        key = jax.random.key(seed)
        ks = jax.random.split(key, 10)
        node_feat = jax.random.normal(ks[0], (N, D), dtype=jnp.float32)
        src = jax.random.randint(ks[1], (E,), 0, N)
        dst = jax.random.randint(ks[2], (E,), 0, N)
        etype = jax.random.randint(ks[3], (E,), 0, R)
        s = 1.0 / np.sqrt(D)
        W_emb = jax.random.normal(ks[4], (D, D), dtype=jnp.float32) * s
        b_emb = jnp.zeros((D,), dtype=jnp.float32)
        bases = jax.random.normal(ks[5], (L, B, D, D), dtype=jnp.float32) * s
        w_coe = jax.random.normal(ks[6], (L, R, B), dtype=jnp.float32) * 0.3
        self_loop = jax.random.normal(ks[7], (L, D, D), dtype=jnp.float32) * s
        bn_gamma = jnp.ones((L, D), dtype=jnp.float32)
        bn_beta = jnp.zeros((L, D), dtype=jnp.float32)
        bn_mean = jnp.zeros((L, D), dtype=jnp.float32)
        bn_var = jnp.ones((L, D), dtype=jnp.float32)
        return {'node_feat': node_feat, 'W_emb': W_emb, 'b_emb': b_emb, 'bases': bases, 'w_coe': w_coe, 'self_loop': self_loop, 'bn_gamma': bn_gamma, 'bn_beta': bn_beta, 'bn_mean': bn_mean, 'bn_var': bn_var, 'src': src, 'dst': dst, 'etype': etype}
    _L0_gnn_all = _L0_gnn_setup()
    _L0_gnn_in = {k: v for k, v in _L0_gnn_all.items() if k in ('W_emb', 'b_emb', 'bases', 'w_coe', 'self_loop', 'bn_gamma', 'bn_beta', 'bn_mean', 'bn_var')}
    del _L0_gnn_all

    def _L1_gnn_setup():
        import jax, jax.numpy as jnp
        import numpy as np
        N_NODES = 6250
        N_EDGES = 100000
        D_FEAT = 128
        key = jax.random.key(seed)
        k1, k2, k3 = jax.random.split(key, 3)
        x = jax.random.normal(k1, (N_NODES, D_FEAT), dtype=jnp.float32)
        edge_src = jnp.sort(jax.random.randint(k2, (N_EDGES,), 0, N_NODES, dtype=jnp.int64))
        edge_dst = jax.random.randint(k3, (N_EDGES,), 0, N_NODES, dtype=jnp.int64)
        return {'x': x, 'edge_src': edge_src, 'edge_dst': edge_dst}
    _L1_gnn_all = _L1_gnn_setup()
    _L1_gnn_in = {k: v for k, v in _L1_gnn_all.items() if k in ()}
    del _L1_gnn_all

    def _L2_gnn_setup():
        import jax, jax.numpy as jnp
        import numpy as np
        N_NODES = 12500
        N_EDGES = 200000
        D = 128
        LEAKY_SLOPE = 0.01
        key = jax.random.key(seed)
        k1, k2, k3, k4 = jax.random.split(key, 4)
        in_states = jax.random.normal(k1, (N_NODES, D), dtype=jnp.float32)
        edges = jax.random.randint(k2, (2, N_EDGES), 0, N_NODES, dtype=jnp.int64)
        W_msg = jax.random.normal(k3, (D, D), dtype=jnp.float32) / np.sqrt(D)
        attn_w = jax.random.normal(k4, (2 * D,), dtype=jnp.float32) / np.sqrt(2 * D)
        W_res = jnp.eye(D, dtype=jnp.float32)
        passthrough_coef = jnp.ones((1,), dtype=jnp.float32)
        return {'in_states': in_states, 'edges': edges, 'W_msg': W_msg, 'attn_w': attn_w, 'W_res': W_res, 'passthrough_coef': passthrough_coef}
    _L2_gnn_all = _L2_gnn_setup()
    _L2_gnn_in = {k: v for k, v in _L2_gnn_all.items() if k in ('W_msg', 'attn_w', 'W_res', 'passthrough_coef')}
    del _L2_gnn_all

    def _L3_gnn_setup():
        import jax, jax.numpy as jnp
        import numpy as np
        NUM_NODES = 6250
        NUM_EDGES = 75000
        D = 128
        key = jax.random.key(seed)
        k1, k2, k3, k4 = jax.random.split(key, 4)
        node_feat = jax.random.normal(k1, (NUM_NODES, D), dtype=jnp.float32)
        edge_feat = jax.random.normal(k2, (NUM_EDGES, D), dtype=jnp.float32)
        src = jax.random.randint(k3, (NUM_EDGES,), 0, NUM_NODES, dtype=jnp.int64)
        dst = jax.random.randint(k4, (NUM_EDGES,), 0, NUM_NODES, dtype=jnp.int64)
        return {'node_feat': node_feat, 'edge_feat': edge_feat, 'src': src, 'dst': dst}
    _L3_gnn_all = _L3_gnn_setup()
    _L3_gnn_in = {k: v for k, v in _L3_gnn_all.items() if k in ()}
    del _L3_gnn_all
    return {'x': x, 'src': src, 'dst': dst, 'edge_attr_128': edge_attr_128, 'edge_type_8': edge_type_8, 'L0_gnn_W_emb': _L0_gnn_in['W_emb'], 'L0_gnn_b_emb': _L0_gnn_in['b_emb'], 'L0_gnn_bases': _L0_gnn_in['bases'], 'L0_gnn_w_coe': _L0_gnn_in['w_coe'], 'L0_gnn_self_loop': _L0_gnn_in['self_loop'], 'L0_gnn_bn_gamma': _L0_gnn_in['bn_gamma'], 'L0_gnn_bn_beta': _L0_gnn_in['bn_beta'], 'L0_gnn_bn_mean': _L0_gnn_in['bn_mean'], 'L0_gnn_bn_var': _L0_gnn_in['bn_var'], 'L2_gnn_W_msg': _L2_gnn_in['W_msg'], 'L2_gnn_attn_w': _L2_gnn_in['attn_w'], 'L2_gnn_W_res': _L2_gnn_in['W_res'], 'L2_gnn_passthrough_coef': _L2_gnn_in['passthrough_coef']}

def reference(x, src, dst, edge_attr_128, edge_type_8, L0_gnn_W_emb, L0_gnn_b_emb, L0_gnn_bases, L0_gnn_w_coe, L0_gnn_self_loop, L0_gnn_bn_gamma, L0_gnn_bn_beta, L0_gnn_bn_mean, L0_gnn_bn_var, L2_gnn_W_msg, L2_gnn_attn_w, L2_gnn_W_res, L2_gnn_passthrough_coef):
    import jax
    import jax.numpy as jnp

    def _L0_gnn_ref(node_feat, W_emb, b_emb, bases, w_coe, self_loop, bn_gamma, bn_beta, bn_mean, bn_var, src, dst, etype):
        import jax, jax.numpy as jnp
        import numpy as np
        N = 6250
        E = 100000
        D = 128
        R = 8
        B = 4
        L = 2
        BN_EPS = 0.001

        def _edge_norm(etype, dst, dtype):
            node_norm = jnp.zeros((N,), dtype=dtype)
            for r in range(R):
                mask = (etype == r).astype(dtype)
                cnt = jax.ops.segment_sum(mask, dst, num_segments=N)
                node_norm = jnp.where(cnt > 0, 1.0 / jnp.maximum(cnt, 1.0), node_norm)
            return node_norm[dst][:, None]
        h = node_feat @ W_emb + b_emb
        norm = _edge_norm(etype, dst, h.dtype)
        for l in range(L):
            W = jnp.einsum('rb,bdf->rdf', w_coe[l], bases[l])
            T = jnp.einsum('nd,rdf->rnf', h, W)
            msg = T[etype, src] * norm
            agg = jax.ops.segment_sum(msg, dst, num_segments=N)
            h = agg + h @ self_loop[l]
            h = bn_gamma[l] * (h - bn_mean[l]) * jax.lax.rsqrt(bn_var[l] + BN_EPS) + bn_beta[l]
            h = jax.nn.relu(h)
        return h

    def _L1_gnn_ref(x, edge_src, edge_dst):
        import jax, jax.numpy as jnp
        import numpy as np
        N_NODES = 6250
        N_EDGES = 100000
        D_FEAT = 128
        neighbor_feats = x[edge_dst]
        agg = jax.ops.segment_sum(neighbor_feats, edge_src, num_segments=N_NODES)
        return x + agg

    def _L2_gnn_ref(in_states, edges, W_msg, attn_w, W_res, passthrough_coef):
        import jax, jax.numpy as jnp
        import numpy as np
        N_NODES = 12500
        N_EDGES = 200000
        D = 128
        LEAKY_SLOPE = 0.01
        n_nodes = in_states.shape[0]
        src, dst = (edges[0], edges[1])
        messages = in_states @ W_msg.T
        s_from = messages @ attn_w[:D]
        s_to = messages @ attn_w[D:]
        e = s_from[src] + s_to[dst]
        e = jnp.where(e >= 0, e, LEAKY_SLOPE * e)
        seg_max = jax.ops.segment_max(e, dst, num_segments=n_nodes)
        e_exp = jnp.exp(e - seg_max[dst])
        seg_sum = jax.ops.segment_sum(e_exp, dst, num_segments=n_nodes)
        alpha = e_exp / seg_sum[dst]
        scaled = alpha[:, None] * messages[src]
        merged = jax.ops.segment_sum(scaled, dst, num_segments=n_nodes)
        new_states_res = jax.nn.relu(merged)
        old_passthrough = in_states @ W_res.T * jax.nn.sigmoid(passthrough_coef[0])
        return old_passthrough + new_states_res

    def _L3_gnn_ref(node_feat, edge_feat, src, dst):
        import jax, jax.numpy as jnp
        import numpy as np
        NUM_NODES = 6250
        NUM_EDGES = 75000
        D = 128
        msg = node_feat[src] + edge_feat
        h_neigh = jax.ops.segment_sum(msg, dst, num_segments=NUM_NODES)
        return h_neigh
    edge_index = jnp.stack([src, dst])
    x = _layernorm(x + _L0_gnn_ref(x, L0_gnn_W_emb, L0_gnn_b_emb, L0_gnn_bases, L0_gnn_w_coe, L0_gnn_self_loop, L0_gnn_bn_gamma, L0_gnn_bn_beta, L0_gnn_bn_mean, L0_gnn_bn_var, src, dst, edge_type_8), axis=-1)
    x = _layernorm(x + _L1_gnn_ref(x, src, dst), axis=-1)
    x = _layernorm(x + _L2_gnn_ref(x, edge_index, L2_gnn_W_msg, L2_gnn_attn_w, L2_gnn_W_res, L2_gnn_passthrough_coef), axis=-1)
    x = _layernorm(x + _L3_gnn_ref(x, edge_attr_128, src, dst), axis=-1)
    return x

_drawn_inputs = setup_inputs


def setup_inputs(seed=0):
    import zlib

    import numpy as np

    out = dict(_drawn_inputs(seed))
    spreads = {'L0_gnn_b_emb': (0.0, 0.1),
     'L0_gnn_bn_gamma': (1.0, 0.2),
     'L0_gnn_bn_beta': (0.0, 0.1),
     'L0_gnn_bn_mean': (0.0, 0.1),
     'L0_gnn_bn_var': (1.0, 0.2)}
    factors = {'L2_gnn_attn_w': 8.0}
    for name, (base, spread) in spreads.items():
        noise = np.random.default_rng([zlib.crc32(name.encode()), seed]).standard_normal(out[name].shape)
        drawn = base * np.exp(spread * noise) if base else spread * noise
        out[name] = jnp.asarray(drawn.astype(out[name].dtype))
    for name, factor in factors.items():
        out[name] = (out[name] * factor).astype(out[name].dtype)
    return out
```

```python
from contextlib import ExitStack

import concourse.bass as bass
from concourse import mybir

ALU = mybir.AluOpType
ACT = mybir.ActivationFunctionType
AX = mybir.AxisListType
F32 = mybir.dt.float32
F16 = mybir.dt.float16
BF16 = mybir.dt.bfloat16
I32 = mybir.dt.int32

P = 128
D = 128
NODES, EDGES = 6250, 206250
RELATIONS, BASES, LAYERS = 8, 4, 2
BN_EPS, LN_EPS, LEAKY = 1e-3, 1e-5, 0.01

NT = -(-NODES // P)
NPAD = NT * P
LAST = NODES - (NT - 1) * P
CHUNK = 64
EPP = 1664
EPAD = P * EPP
CPP = EPP // CHUNK
CHUNKS = EPAD // CHUNK
REAL_CHUNKS = -(-EDGES // CHUNK)
PAD_DST = 8192

GROUPS, PER = 7, 5
SLOTS = GROUPS * PER
TILE_STEP = SLOTS * P // CHUNK
WIN = 8
NW = NPAD // WIN
WPT = P // WIN
WSLOTS = 3
WIN_STEP = WSLOTS * P // CHUNK
WGROUPS = 7
WPG = NW // WGROUPS
REC = 5
TW = RELATIONS * D
GW = 2 * D + RELATIONS
WC = NT * WIN
SEG = 7
SW = SEG * P
NSEG = NT // SEG
HALF = NSEG * SW // 2
HSEG = HALF // NSEG
FAR = -3.0e38

assert NT == SEG * NSEG and EPAD - REAL_CHUNKS * CHUNK >= SLOTS * P


class Kernel:
    pass


def spread(ap, n):
    return ap.unsqueeze(len(ap.shape)).to_broadcast([*ap.shape, n])


def repeat(ap, n):
    return ap.unsqueeze(1).to_broadcast([ap.shape[0], n, ap.shape[1]])


def build(nc, ins, out, stop=9, debug=None):
    k = Kernel()
    dram = lambda name, shape, dt=F32: nc.dram_tensor(name, shape, dt, kind="Internal").ap()
    k.rec_d = dram("edge_records", (EPAD * REC,))
    k.chunk_d = dram("chunk_bounds", (2, CHUNKS))
    k.wspan_d = dram("window_spans", (NW,))
    k.wlo_d = dram("window_starts", (NW,), I32)
    k.tile_d = dram("tile_starts_and_spans", (2, NT), I32)
    k.table_d = [dram(f"table_{l}", (NPAD * RELATIONS, D)) for l in range(LAYERS)]
    k.cs_d = dram("counts_by_source", (NT, P, NPAD))
    k.cd_d = dram("counts_by_destination", (NT, P, NPAD))
    k.pen_d = dram("no_edge_penalty", (NT, P, NPAD), BF16)
    k.attr_d = dram("attribute_sums", (P, NPAD))
    k.ins, k.out = ins, out
    with ExitStack() as ctx:
        sb = lambda name, shape, dt=F32: ctx.enter_context(nc.sbuf_tensor(name, shape, dt))
        k.vars_made = ctx.enter_context(nc.semaphore("variances_made"))
        k.roots_made = ctx.enter_context(nc.semaphore("roots_made"))
        both = sb("state_and_spare", [P, 2 * NPAD + NT])
        k.pair = both[:, 0:2 * NPAD].rearrange("p (a t f) -> p a t f", a=2, f=D)
        k.x, k.spare = k.pair[:, 0], k.pair[:, 1]
        k.msg = both[:, NPAD:].rearrange("p (t f) -> p t f", f=D + 1)
        k.self_ = sb("self_term", [P, NT, D])
        k.ident = sb("ident", [P, P])
        k.lneps = sb("ln_eps", [P, 1])
        k.stat = sb("stat", [P, 6])
        k.stat7 = sb("stat_of_seven", [P, SEG, 6])
        k.mv7 = sb("mean_var_of_seven", [P, SEG, 2])
        k.mv1 = sb("mean_var_of_tile", [P, 2])
        k.mv = sb("mean_var", [P, NT, 2])
        k.rstd = sb("rstd", [P, NT])
        with ExitStack() as layers:
            inner = lambda name, shape, dt=F32: layers.enter_context(nc.sbuf_tensor(name, shape, dt))
            k.attr = inner("attr_sum", [P, NT, D])
            k.rank8 = inner("rank8", [P, RELATIONS])
            k.iota8 = inner("iota8", [P, RELATIONS])
            k.iota16 = inner("iota16", [P, WC], F16)
            k.iota = inner("iota", [P, P])
            k.wbase = inner("window_base", [P, NT, WPT])
            k.tbase = inner("minus_tile_base", [P, NT])
            k.wr = inner("relation_weights", [P, LAYERS, TW])
            k.loop = inner("loop_weights", [P, LAYERS, D])
            k.bns = inner("bn_scale", [P, LAYERS, D])
            k.bnb = inner("bn_shift", [P, LAYERS, D])
            k.norm = inner("norm", [P, NT])
            k.tlo = inner("tile_start_row", [1, NT], I32)
            k.tspan = inner("tile_span_row", [1, NT], I32)
            k.wlo = inner("window_start_row", [1, NW], I32)
            phase_prepare(nc, k)
            if stop >= 2:
                phase_layer(nc, k, 0)
            if stop >= 3:
                phase_layer(nc, k, 1)
        if stop >= 4:
            phase_sum_to_source(nc, k)
        if stop >= 5:
            phase_attention(nc, k)
        if stop >= 6:
            phase_edge_sum(nc, k)
        if debug:
            debug(nc, k)


def phase_prepare(nc, k):
    with ExitStack() as ctx:
        sb = lambda name, shape, dt=F32: ctx.enter_context(nc.sbuf_tensor(name, shape, dt))
        sem = lambda name: ctx.enter_context(nc.semaphore("p_" + name))
        a = k.ins
        work = sb("work", [P, 5 * CHUNKS])
        src, dst, typ, itmp = (work[:, i * EPP:(i + 1) * EPP].bitcast(I32) for i in range(4))
        dstf = work[:, 4 * EPP:5 * EPP]
        rec = work[:, 5 * EPP:(5 + REC) * EPP].rearrange("p (e w) -> p e w", w=REC)
        bounds = work[:, 0:2 * CHUNKS].rearrange("p (m c) -> p m c", m=2)
        scr = work[:, 2 * CHUNKS:4 * CHUNKS].rearrange("p (m c) -> p m c", m=2)
        asc = work[:, 4 * CHUNKS:5 * CHUNKS]
        desc = k.attr[:, :, :].rearrange("p t f -> p (t f)")[:, 0:CHUNKS]
        cm = sb("chunk_min_max", [P, 2, CPP])
        lob = sb("lob", [P, WGROUPS + 1])
        hib = sb("hib", [P, WGROUPS + 1])
        m1 = sb("m1", [P, WGROUPS + 1])
        m2 = sb("m2", [P, WGROUPS + 1])
        wsp = sb("wsp", [P, WGROUPS + 1])
        loi = sb("loi", [P, WGROUPS + 1], I32)
        wt = sb("wt", [NT, WPT])
        smax = sb("smax", [NT, 1])
        smaxf = sb("smaxf", [NT, 1])
        smaxi = sb("smaxi", [NT, 1], I32)
        wemb = sb("wemb", [P, D])
        bemb = sb("bemb", [P, 1])
        bases = sb("bases", [P, LAYERS, BASES, D])
        coe = sb("coe", [P, LAYERS * RELATIONS * BASES])
        bn = [sb(f"bn{i}", [P, LAYERS, D]) for i in range(4)]
        eps = sb("eps", [P, 1])
        identz = sb("identz", [P, P])
        xt = k.x[:, :, :].rearrange("p t f -> p (t f)")
        ht = sb("ht", [P, SW])
        tsb = sb("tsb", [P, 2, TW])
        ph = ctx.enter_context(nc.psum_tensor("ph", [P, 1024], F32))
        pt = ctx.enter_context(nc.psum_tensor("pt", [P, 2, 1024], F32))
        pse = ctx.enter_context(nc.psum_tensor("pse", [P, 2, 512], F32))

        edges_in, weights_in, x_in = sem("edges_in"), sem("weights_in"), sem("x_in")
        CONSTS = 16
        consts, rec_made, rec_out = sem("consts"), sem("rec_made"), sem("rec_out")
        chunk_out, bounds_in = sem("chunk_out"), sem("bounds_in")
        spans_made, spans_out, spans_in = sem("spans_made"), sem("spans_out"), sem("spans_in")
        tiles_made, tiles_out, rows_in = sem("tiles_made"), sem("tiles_out"), sem("rows_in")
        wr_made, var_made = sem("wr_made"), sem("var_made")
        ht_ps, ht_sb, t_ps, t_sb = sem("ht_ps"), sem("ht_sb"), sem("t_ps"), sem("t_sb")
        t_out = sem("t_out")
        t_bank, t_free = sem("t_bank"), sem("t_free")
        block = ctx.enter_context(nc.Block())

        @block.sync
        def _(e):
            for t, name in ((dst, "dst"), (src, "src"), (typ, "edge_type_8")):
                e.dma_start(t, a[name].rearrange("(p c) -> p c", p=P)).then_inc(edges_in, 16)
            e.dma_start(xt, a["x_transposed"]).then_inc(x_in, 16)
            e.wait_ge(rec_made, 1)
            e.dma_start(k.chunk_d.rearrange("m (p c) -> p m c", p=P), cm[:, :, :]).then_inc(chunk_out, 16)
            e.wait_ge(rec_made, 2)
            e.dma_start(k.rec_d.rearrange("(p c) -> p c", p=P), work[:, 5 * EPP:(5 + REC) * EPP]).then_inc(rec_out, 16)
            e.wait_ge(chunk_out, 16)
            e.wait_ge(rec_out, 16)
            e.dma_start(work[:, 0:2 * CHUNKS], k.chunk_d.rearrange("m c -> (m c)").partition_broadcast(P))\
             .then_inc(bounds_in, 16)
            e.wait_ge(spans_made, 1)
            e.dma_start(k.wspan_d.rearrange("(g p) -> p g", p=WPG), wsp[0:WPG, 0:WGROUPS],
                        allow_slow_non_contiguous=True).then_inc(spans_out, 16)
            e.dma_start(k.wlo_d.rearrange("(g p) -> p g", p=WPG), loi[0:WPG, 0:WGROUPS],
                        allow_slow_non_contiguous=True).then_inc(spans_out, 16)
            e.wait_ge(spans_out, 32)
            e.dma_start(wt[:, :], k.wspan_d.rearrange("(t q) -> t q", q=WPT)).then_inc(spans_in, 16)
            e.dma_start(k.wlo[:, :], k.wlo_d.rearrange("(a w) -> a w", a=1)).then_inc(rows_in, 16)
            e.wait_ge(tiles_made, 1)
            e.dma_start(k.tile_d[0:1, :].rearrange("a t -> t a"), loi[0:NT, WGROUPS:WGROUPS + 1])\
             .then_inc(tiles_out, 16)
            e.dma_start(k.tile_d[1:2, :].rearrange("a t -> t a"), smaxi[:, :]).then_inc(tiles_out, 16)
            e.wait_ge(tiles_out, 32)
            e.dma_start(k.tlo[:, :], k.tile_d[0:1, :]).then_inc(rows_in, 16)
            e.dma_start(k.tspan[:, :], k.tile_d[1:2, :]).then_inc(rows_in, 16)
            e.wait_ge(rows_in, 48)

        @block.gpsimd
        def _(e):
            e.memset(identz[:, :], 0.0).then_inc(consts, 1)
            e.iota(k.iota[:, :], [[1, P]], base=0, channel_multiplier=0, allow_small_or_imprecise_dtypes=True)\
             .then_inc(consts, 1)
            e.iota(lob[:, 0:WGROUPS], [[WIN * WPG, WGROUPS]], base=0, channel_multiplier=WIN,
                   allow_small_or_imprecise_dtypes=True).then_inc(consts, 1)
            e.iota(hib[:, 0:WGROUPS], [[WIN * WPG, WGROUPS]], base=WIN - 1, channel_multiplier=WIN,
                   allow_small_or_imprecise_dtypes=True).then_inc(consts, 1)
            e.iota(lob[:, WGROUPS:], [[0, 1]], base=0, channel_multiplier=P,
                   allow_small_or_imprecise_dtypes=True).then_inc(consts, 1)
            e.iota(hib[:, WGROUPS:], [[0, 1]], base=P - 1, channel_multiplier=P,
                   allow_small_or_imprecise_dtypes=True).then_inc(consts, 1)
            e.memset(eps[:, :], BN_EPS).then_inc(consts, 1)
            e.wait_ge(consts, 7)
            e.affine_select(out=k.ident[:, :], in_=identz[:, :], compare_op=ALU.not_equal, fill=1.0, base=0,
                            pattern=[[-1, P]], channel_multiplier=1).then_inc(consts, 1)
            e.iota(desc, [[-1, CHUNKS]], base=CHUNKS, channel_multiplier=0,
                   allow_small_or_imprecise_dtypes=True).then_inc(consts, 1)
            e.iota(k.iota16[:, :], [[1, WC]], base=0, channel_multiplier=0,
                   allow_small_or_imprecise_dtypes=True).then_inc(consts, 1)
            e.iota(k.iota8[:, :], [[1, RELATIONS]], base=0, channel_multiplier=0,
                   allow_small_or_imprecise_dtypes=True).then_inc(consts, 1)
            e.iota(k.rank8[:, :], [[1, RELATIONS]], base=1, channel_multiplier=0,
                   allow_small_or_imprecise_dtypes=True).then_inc(consts, 1)
            e.memset(k.lneps[:, :], LN_EPS).then_inc(consts, 1)
            e.iota(k.wbase[:, :, :].rearrange("p t q -> p (t q)"), [[WIN, NW]], base=0, channel_multiplier=0,
                   allow_small_or_imprecise_dtypes=True).then_inc(consts, 1)
            e.iota(k.tbase[:, :], [[-P, NT]], base=0, channel_multiplier=0,
                   allow_small_or_imprecise_dtypes=True).then_inc(consts, 1)
            e.wait_ge(rec_out, 16)
            e.iota(asc, [[1, CHUNKS]], base=1, channel_multiplier=0,
                   allow_small_or_imprecise_dtypes=True).then_inc(consts, 1)
            e.sem_inc(t_free, 2)
            with e.Fori(0, NT) as t:
                e.wait_ge(t_sb, t + 1)
                e.dma_start(k.table_d[0][bass.ts(t, P * RELATIONS), :].rearrange("(p r) f -> p (r f)", r=RELATIONS),
                            tsb[:, bass.ds(t & 1, 1), :]).then_inc(t_out, 16)
                e.wait_ge(t_out, (t + 1) * 16)
                e.sem_inc(t_free, 1)

        @block.scalar
        def _(e):
            for t, ap in ((wemb[:, :], a["L0_gnn_W_emb"]),
                          (bemb[:, :], a["L0_gnn_b_emb"].rearrange("(p a) -> p a", a=1)),
                          (bases[:, :, :, :], a["L0_gnn_bases"].rearrange("l b d f -> d l b f")),
                          (coe[:, :], a["L0_gnn_w_coe"].rearrange("l r b -> (l r b)").partition_broadcast(P)),
                          (k.loop[:, :, :], a["L0_gnn_self_loop"].rearrange("l d f -> d l f")),
                          *((bn[i][:, :, :], a["L0_gnn_bn_" + n].rearrange("l f -> (l f)").partition_broadcast(P)
                             .rearrange("p (l f) -> p l f", l=LAYERS))
                            for i, n in enumerate(("gamma", "beta", "mean", "var")))):
                e.dma_start(t, ap).then_inc(weights_in, 16)
            e.wait_ge(weights_in, 9 * 16)
            e.wait_ge(consts, 7)
            e.activation(bn[3][:, :, :], bn[3][:, :, :], ACT.Sqrt, bias=eps[:, 0:1]).then_inc(var_made, 1)
            with e.Fori(0, NSEG) as tb:
                e.wait_ge(ht_ps, tb + 1)
                e.wait_ge(t_ps, tb * SEG)
                e.activation(ht[:, :], ph[:, 0:SW], ACT.Identity, bias=bemb[:, 0:1]).then_inc(ht_sb, 1)
                for i in range(SEG):
                    t = tb * SEG + i
                    e.wait_ge(t_ps, t + 1)
                    e.wait_ge(t_free, t + 1)
                    e.activation(tsb[:, bass.ds(t & 1, 1), :], pt[:, bass.ds(t & 1, 1), :], ACT.Copy)
                    e.activation(k.self_[:, bass.ds(t, 1), :], pse[:, bass.ds(t & 1, 1), 0:D], ACT.Copy)
                    e.drain().then_inc(t_sb, 1)
                    e.sem_inc(t_bank, 1)

        @block.tensor
        def _(e):
            e.wait_ge(x_in, 16)
            e.wait_ge(weights_in, 9 * 16)
            e.sem_inc(t_bank, 2)
            with e.Fori(0, NSEG) as tb:
                e.wait_ge(ht_sb, tb)
                for h in range(2):
                    m = e.matmul(ph[:, h * 512:h * 512 + (512, SW - 512)[h]], wemb[:, :],
                                 xt[:, bass.ds(tb * SW + h * 512, (512, SW - 512)[h])], start=True, stop=True)
                m.then_inc(ht_ps, 1)
                e.wait_ge(ht_sb, tb + 1)
                e.wait_ge(wr_made, 1)
                for i in range(SEG):
                    t = tb * SEG + i
                    e.wait_ge(t_bank, t + 1)
                    for h in range(2):
                        e.matmul(pt[:, bass.ds(t & 1, 1), h * 512:(h + 1) * 512], ht[:, i * P:(i + 1) * P],
                                 k.wr[:, 0, h * 512:(h + 1) * 512], start=True, stop=True)
                    e.matmul(pse[:, bass.ds(t & 1, 1), 0:D], ht[:, i * P:(i + 1) * P], k.loop[:, 0, :],
                             start=True, stop=True).then_inc(t_ps, 1)

        @block.vector
        def _(e):
            e.wait_ge(edges_in, 48)
            e.tensor_copy(dstf, dst)
            e.tensor_scalar(itmp, src, P - 1, None, ALU.bitwise_and)
            e.drain()
            for m, op in enumerate((ALU.min, ALU.max)):
                e.tensor_reduce(cm[:, m, :], dstf.rearrange("p (c i) -> p c i", i=CHUNK), AX.X, op)
            e.tensor_copy(rec[:, :, 0], dstf)
            e.tensor_copy(rec[:, :, 1], itmp)
            e.tensor_copy(rec[:, :, 3], typ)
            e.drain().then_inc(rec_made, 1)
            e.tensor_scalar(itmp, src, 7, 3, ALU.logical_shift_right, ALU.logical_shift_left)
            e.tensor_scalar(dst, src, 3, None, ALU.logical_shift_left)
            e.drain()
            e.tensor_copy(rec[:, :, 2], itmp)
            e.tensor_tensor(rec[:, :, 4].bitcast(I32), dst, typ, ALU.bitwise_or)
            e.drain().then_inc(rec_made, 1)
            e.wait_ge(weights_in, 9 * 16)
            for b in range(BASES):
                for l in range(LAYERS):
                    for r in range(RELATIONS):
                        w = k.wr[:, l, r * D:(r + 1) * D]
                        c = coe[:, (l * RELATIONS + r) * BASES + b:(l * RELATIONS + r) * BASES + b + 1]
                        if b == 0:
                            e.tensor_scalar(w, bases[:, l, b, :], c, None, ALU.mult)
                        else:
                            e.scalar_tensor_tensor(w, bases[:, l, b, :], c, w, ALU.mult, ALU.add)
                e.drain()
            e.sem_inc(wr_made, 1)
            e.wait_ge(var_made, 1)
            e.reciprocal(bn[3][:, :, :], bn[3][:, :, :])
            e.drain()
            e.tensor_tensor(k.bns[:, :, :], bn[0][:, :, :], bn[3][:, :, :], ALU.mult)
            e.drain()
            e.tensor_tensor(bn[2][:, :, :], bn[2][:, :, :], k.bns[:, :, :], ALU.mult)
            e.drain()
            e.tensor_tensor(k.bnb[:, :, :], bn[1][:, :, :], bn[2][:, :, :], ALU.subtract)
            e.wait_ge(bounds_in, 16)
            e.wait_ge(consts, CONSTS)
            for g in range(WGROUPS + 1):
                e.scalar_tensor_tensor(scr[:, 0, :], bounds[:, 1, :], lob[:, g:g + 1], desc, ALU.is_ge, ALU.mult)
                e.scalar_tensor_tensor(scr[:, 1, :], bounds[:, 0, :], hib[:, g:g + 1], asc, ALU.is_le, ALU.mult)
                e.drain()
                e.reduce_max(m1[:, g:g + 1], scr[:, 0, :], AX.X)
                e.reduce_max(m2[:, g:g + 1], scr[:, 1, :], AX.X)
                e.drain()
            e.tensor_scalar(m1[:, :], m1[:, :], -1.0, float(CHUNKS), ALU.mult, ALU.add)
            e.drain()
            e.tensor_scalar(m1[:, :], m1[:, :], float(REAL_CHUNKS), None, ALU.min)
            e.drain()
            e.tensor_copy(loi[:, :], m1[:, :])
            e.tensor_tensor(wsp[:, :], m2[:, :], m1[:, :], ALU.subtract)
            e.drain().then_inc(spans_made, 1)
            e.wait_ge(spans_in, 16)
            e.reduce_max(smax[:, :], wt[:, :], AX.X)
            e.tensor_scalar(wsp[0:NT, WGROUPS:], wsp[0:NT, WGROUPS:], float(WIN_STEP), None, ALU.mult)
            e.drain()
            e.tensor_scalar(smax[:, :], smax[:, :], float(TILE_STEP), 1.0, ALU.mult, ALU.max)
            e.drain()
            e.tensor_tensor(smaxf[:, :], smax[:, :], wsp[0:NT, WGROUPS:], ALU.max)
            e.drain()
            e.tensor_copy(smaxi[:, :], smaxf[:, :])
            e.drain().then_inc(tiles_made, 1)


WINDOWS = [2, 2, 2, 2, 2, 3, 3]


def counter(e, name):
    r = e.alloc_register(name)
    e.reg_mov(r, 0)
    return r


def phase_layer(nc, k, l):
    with ExitStack() as ctx:
        sb = lambda name, shape, dt=F32: ctx.enter_context(nc.sbuf_tensor(f"{name}_{l}", shape, dt))
        pb = lambda name, shape, dt=F32: ctx.enter_context(nc.psum_tensor(f"{name}_{l}", shape, dt))
        sem = lambda name: ctx.enter_context(nc.semaphore(f"l{l}_{name}"))
        first = l == 0
        gw = GW if first else D
        recs = sb("recs", [P, SLOTS, REC])
        rows = sb("rows", [P, SLOTS, gw])
        hot = sb("hot", [P, SLOTS, P])
        agg = sb("agg", [P, gw])
        h = sb("h", [P, D])
        acc = pb("acc", [P, 512])
        rec_in = [sem(f"rec_in{g}") for g in range(GROUPS)]
        gathered = [sem(f"gathered{g}") for g in range(GROUPS)]
        turn = sem("turn")
        ring, hot_made, acc_free = sem("ring"), sem("hot_made"), sem("acc_free")
        if first:
            wrec = sb("wrec", [P, WPT * WSLOTS, REC])
            key = sb("key", [P, WPT * WSLOTS])
            dloc = sb("dloc", [P, WPT * WSLOTS])
            inw = sb("inw", [P, WPT * WSLOTS])
            wlo = sb("wlo16", [P, WPT * WSLOTS])
            whot = sb("whot", [P, 4, WSLOTS, P], F16)
            wkey = sb("wkey", [P, 4, WSLOTS, WC], F16)
            cs = k.pair
            small = sb("small", [P, 4, RELATIONS])
            best = sb("best", [P, 1])
            ht = sb("ht", [P, P])
            tsb = sb("tsb", [P, TW])
            wps = pb("wps", [P, 4, 512])
            pm = pb("pm", [P, 512])
            pt = pb("pt", [P, 1024])
            attr_in = [sem(f"attr_in{g}") for g in range(GROUPS)]
            wrec_in, keys_made, whot_made = sem("wrec_in"), sem("keys_made"), sem("whot_made")
            counted, moved, stored, summed = sem("counted"), sem("moved"), sem("stored"), sem("summed")
            h_made, ht_ps, ht_sb = sem("h_made"), sem("ht_ps"), sem("ht_sb")
            t_ps, t_sb, t_out = sem("t_ps"), sem("t_sb"), sem("t_out")
        else:
            csr = sb("csr", [P, NSEG, SW])
            cdr = k.spare.rearrange("p t f -> p (t f)").rearrange("p (g c) -> p g c", g=NSEG)
            pen = sb("pen", [P, NSEG, SW], BF16)
            tps = pb("tps", [P, 3, 1024])
            cs_in = [sem(f"cs_in{g}") for g in range(GROUPS)]
            stored = [sem(f"stored{g}") for g in range(GROUPS)]
            turned, moved, pen_made, x_in = sem("turned"), sem("moved"), sem("pen_made"), sem("x_in")
            attr_out = sem("attr_out")
        block = ctx.enter_context(nc.Block())

        def rounds(e, body, before=None, after=None):
            done = counter(e, f"rounds_{l}")
            with e.Fori(0, NT) as t:
                if before:
                    before(t)
                span = e.value_load(k.tspan[0:1, bass.ds(t, 1)], min_val=1, max_val=CHUNKS * TILE_STEP)
                with e.Fori(0, span, WIN_STEP * TILE_STEP) as r:
                    body(t, r, e.snap(done, min_val=0, max_val=1 << 20))
                    e.reg_add(done, done, 1)
                if after:
                    after(t)
            return e.snap(done, min_val=0, max_val=1 << 20)

        @block.sync
        def _(e):
            if not first:
                e.dma_start(k.x[:, :, :], k.ins["x"].rearrange("(t p) f -> p t f", p=P)).then_inc(x_in, 16)
                e.dma_start(k.attr_d, k.attr[:, :, :].rearrange("p t f -> p (t f)")).then_inc(attr_out, 16)
            at = e.alloc_register(f"tile_chunk_{l}")
            wat = e.alloc_register(f"window_offset_{l}")
            wch = e.alloc_register(f"window_chunk_{l}")

            def before(t):
                e.reg_mov(at, e.value_load(k.tlo[0:1, bass.ds(t, 1)], min_val=0, max_val=REAL_CHUNKS))
                e.reg_mov(wat, 0)

            def body(t, r, b):
                if first:
                    for q in range(WPT):
                        lo = e.value_load(k.wlo[0:1, bass.ds(t * WPT + q, 1)], min_val=0, max_val=REAL_CHUNKS)
                        e.reg_mov(wch, lo)
                        e.reg_add(wch, wch, wat)
                        e.reg_alu(wch, wch, CHUNKS - WIN_STEP, ALU.min)
                        c = e.snap(wch, min_val=0, max_val=CHUNKS - WIN_STEP)
                        e.wait_ge(keys_made, b)
                        e.dma_start(wrec[:, q * WSLOTS:(q + 1) * WSLOTS, :].rearrange("p a b -> p (a b)"),
                                    k.rec_d[bass.ds(c * (CHUNK * REC), P * WSLOTS * REC)]
                                    .rearrange("(p c) -> p c", p=P)).then_inc(wrec_in, 16)
                    e.reg_add(wat, wat, WIN_STEP)
                c = e.snap(at, min_val=0, max_val=REAL_CHUNKS)
                for g in range(GROUPS):
                    e.wait_ge(ring, b * GROUPS + (g + 1))
                    s = slice(g * PER, (g + 1) * PER)
                    e.dma_start(recs[:, s, :].rearrange("p a b -> p (a b)"),
                                k.rec_d[bass.ds(c * (CHUNK * REC), P * SLOTS * REC)]
                                .rearrange("(p c) -> p c", p=P)[:, g * PER * REC:(g + 1) * PER * REC])\
                     .then_inc(rec_in[g], 16)
                    if first:
                        e.dma_start(rows[:, s, D:2 * D],
                                    k.ins["edge_attr_128"][bass.ds(c * CHUNK, P * SLOTS), :]
                                    .rearrange("(p j) f -> p j f", p=P)[:, s, :]).then_inc(attr_in[g], 16)
                    else:
                        e.wait_ge(turned, b * GROUPS + (g + 1))
                        e.dma_start(csr[:, g, :], k.cs_d[bass.ds(t, 1), :, g * SW:(g + 1) * SW]
                                    .rearrange("a p c -> (a p) c")).then_inc(cs_in[g], 16)
                e.reg_add(at, at, TILE_STEP)
                e.reg_alu(at, at, REAL_CHUNKS, ALU.min)

            rounds(e, body, before)
            if not first:
                e.wait_ge(attr_out, 16)

        @block.gpsimd
        def _(e):
            def body(t, r, b):
                for g in range(GROUPS):
                    e.wait_ge(rec_in[g], (b + 1) * 16)
                    e.wait_ge(ring, b * GROUPS + (g + 1))
                    e.sem_inc(turn, 1)
                    for j in range(g * PER, (g + 1) * PER):
                        e.indirect_dma_start(
                            out=rows[:, j, 0:D], out_offset=None, in_=k.table_d[l],
                            in_offset=bass.IndirectOffsetOnAxis(ap=recs[:, j, 4:5].bitcast(I32), axis=0),
                        ).then_inc(gathered[g], 16)

            rounds(e, body)

        @block.tensor
        def _(e):
            e.sem_inc(ring, GROUPS)
            if first:
                e.sem_inc(counted, 4)
            else:
                e.sem_inc(turned, GROUPS)

            def body(t, r, b):
                q = 0
                for g in range(GROUPS):
                    e.wait_ge(gathered[g], (b + 1) * (16 * PER))
                    e.wait_ge(hot_made, b * GROUPS + (g + 1))
                    if first:
                        e.wait_ge(attr_in[g], (b + 1) * 16)
                    if g == 0:
                        e.wait_ge(acc_free, b)
                    for j in range(g * PER, (g + 1) * PER):
                        m = e.matmul(acc[:, 0:gw], hot[:, j, :], rows[:, j, :], start=j == 0, stop=j == SLOTS - 1)
                    m.then_inc(ring, 1)
                    if not first:
                        e.wait_ge(cs_in[g], (b + 1) * 16)
                        e.wait_ge(moved, b * GROUPS + max(0, g - 2))
                        for i in range(SEG):
                            m = e.transpose(tps[:, g % 3, i * P:(i + 1) * P], csr[:, g, i * P:(i + 1) * P], k.ident[:, :])
                        m.then_inc(turned, 1)
                        continue
                    for _ in range(WINDOWS[g]):
                        e.wait_ge(whot_made, b * WPT + (q + 1))
                        e.wait_ge(moved, b * WPT + (q + 1))
                        for j in range(WSLOTS):
                            m = e.matmul(wps[:, q % 4, 0:WC], whot[:, q % 4, j, :], wkey[:, q % 4, j, :],
                                         start=j == 0, stop=j == WSLOTS - 1)
                        m.then_inc(counted, 1)
                        q += 1

            def after(t):
                e.wait_ge(h_made, t + 1)
                e.wait_ge(t_sb, t)
                e.transpose(pm[:, 0:P], h[:, :], k.ident[:, :]).then_inc(ht_ps, 1)
                e.wait_ge(ht_sb, t + 1)
                for i in range(2):
                    e.matmul(pt[:, i * 512:(i + 1) * 512], ht[:, :], k.wr[:, 1, i * 512:(i + 1) * 512],
                             start=True, stop=True)
                e.matmul(pm[:, P:2 * P], ht[:, :], k.loop[:, 1, :], start=True, stop=True).then_inc(t_ps, 1)

            rounds(e, body, after=after if first else None)

        @block.scalar
        def _(e):
            if first:
                e.sem_inc(moved, 4)

            def body(t, r, b):
                if not first:
                    for g in range(GROUPS):
                        e.wait_ge(turned, b * GROUPS + (g + 1 + GROUPS))
                        e.wait_ge(stored[g], b * 32)
                        e.wait_ge(pen_made, b * GROUPS + (g + 1))
                        e.activation(cdr[:, g, :], tps[:, g % 3, 0:SW], ACT.Copy).then_inc(moved, 1)
                        e.wait_ge(moved, b * GROUPS + (g + 1))
                        e.dma_start(k.cd_d[bass.ds(t, 1), :, g * SW:(g + 1) * SW].rearrange("a p c -> (a p) c"),
                                    cdr[:, g, :]).then_inc(stored[g], 16)
                        e.wait_ge(pen_made, b * GROUPS + (g + 1 + GROUPS))
                        e.dma_start(k.pen_d[bass.ds(t, 1), :, g * SW:(g + 1) * SW].rearrange("a p c -> (a p) c"),
                                    pen[:, g, :]).then_inc(stored[g], 16)
                    return
                for q in range(WPT):
                    e.wait_ge(counted, b * WPT + (q + 1 + 4))
                    e.activation(cs[:, bass.ds(b & 1, 1), :, q * WIN:(q + 1) * WIN].rearrange("p a c w -> p (a c) w"),
                                 wps[:, q % 4, 0:WC].rearrange("p (c w) -> p c w", w=WIN), ACT.Copy).then_inc(moved, 1)
                e.wait_ge(moved, b * WPT + (WPT + 4))
                e.wait_ge(summed, b + 1)
                e.wait_ge(stored, b * 16)
                e.dma_start(k.cs_d[bass.ds(t, 1), :, :].rearrange("a p c -> (a p) c"),
                            cs[:, bass.ds(b & 1, 1), :, :].rearrange("p a t d -> p (a t d)")).then_inc(stored, 16)

            def after(t):
                e.wait_ge(ht_ps, t + 1)
                e.activation(ht[:, :], pm[:, 0:P], ACT.Copy).then_inc(ht_sb, 1)
                e.wait_ge(t_ps, t + 1)
                e.wait_ge(t_out, t * 16)
                e.activation(tsb[:, :], pt[:, :], ACT.Copy)
                e.activation(k.self_[:, bass.ds(t, 1), :], pm[:, P:2 * P], ACT.Copy).then_inc(t_sb, 1)
                e.wait_ge(t_sb, t + 1)
                e.dma_start(k.table_d[1][bass.ts(t, P * RELATIONS), :].rearrange("(p r) f -> p (r f)", r=RELATIONS),
                            tsb[:, :]).then_inc(t_out, 16)

            total = rounds(e, body, after=after if first else None)
            if first:
                e.wait_ge(t_out, NT * 16)
                e.wait_ge(stored, total * 16)
            else:
                for g in range(GROUPS):
                    e.wait_ge(stored[g], total * 32)
                roots(e, k, 1)
            e.sem_inc(turn, 1)

        @block.vector
        def _(e):
            if not first:
                e.sem_inc(pen_made, GROUPS)
                e.wait_ge(x_in, 16)

            def before(t):
                e.memset(agg[:, :], 0.0)

            def keys(t, b):
                e.wait_ge(wrec_in, (b + 1) * (16 * WPT))
                dl = dloc[:, :].rearrange("p (q j) -> p q j", j=WSLOTS)
                e.tensor_tensor(dl, wrec[:, :, 0].rearrange("p (q j) -> p q j", j=WSLOTS),
                                spread(k.wbase[:, bass.ds(t, 1), :].rearrange("p a q -> p (a q)"), WSLOTS), ALU.subtract)
                e.tensor_copy(wlo[:, :], wrec[:, :, 1])
                e.drain()
                e.tensor_scalar(inw[:, :], dloc[:, :], 0.0, None, ALU.is_ge)
                e.scalar_tensor_tensor(key[:, :], dloc[:, :], 1.0, wrec[:, :, 2], ALU.add, ALU.add)
                e.drain()
                e.scalar_tensor_tensor(inw[:, :], dloc[:, :], float(WIN), inw[:, :], ALU.is_lt, ALU.mult)
                e.drain()
                e.tensor_tensor(key[:, :], key[:, :], inw[:, :], ALU.mult)
                e.drain()
                e.tensor_scalar(key[:, :], key[:, :], -1.0, None, ALU.add)
                e.drain().then_inc(keys_made, 1)

            def body(t, r, b):
                if first:
                    keys(t, b)
                q = 0
                base = k.tbase[:, bass.ds(t, 1)]
                for g in range(GROUPS):
                    e.wait_ge(rec_in[g], (b + 1) * 16)
                    e.wait_ge(ring, b * GROUPS + (g + 1))
                    for j in range(g * PER, (g + 1) * PER):
                        m = e.tensor_scalar(hot[:, j, :], k.iota[:, :], recs[:, j, 0:1], base,
                                            ALU.subtract, ALU.is_equal)
                    if first:
                        s = slice(g * PER, (g + 1) * PER)
                        m = e.tensor_tensor(rows[:, s, 2 * D:], repeat(k.iota8[:, :], PER),
                                            spread(recs[:, s, 3], RELATIONS), ALU.is_equal)
                    m.then_inc(hot_made, 1)
                    if not first:
                        e.wait_ge(moved, b * GROUPS + (g + 1))
                        e.tensor_scalar(pen[:, g, :], cdr[:, g, :], 0.0, FAR, ALU.is_equal, ALU.mult)\
                         .then_inc(pen_made, 1)
                        continue
                    for _ in range(WINDOWS[g]):
                        e.wait_ge(counted, b * WPT + (q + 1))
                        for j in range(WSLOTS):
                            i = q * WSLOTS + j
                            e.tensor_scalar(whot[:, q % 4, j, :], k.iota16[:, 0:P], wlo[:, i:i + 1], None, ALU.is_equal)
                            m = e.tensor_scalar(wkey[:, q % 4, j, :], k.iota16[:, :], key[:, i:i + 1], None, ALU.is_equal)
                        m.then_inc(whot_made, 1)
                        q += 1
                e.drain()
                e.wait_ge(ring, b * GROUPS + 2 * GROUPS)
                e.tensor_tensor(agg[:, :], agg[:, :], acc[:, 0:gw], ALU.add).then_inc(acc_free, 1)
                if first:
                    with e.If(r > 0):
                        e.wait_ge(moved, b * WPT + (WPT + 4))
                        mine = cs[:, bass.ds(b & 1, 1), :, :].rearrange("p a t d -> p (a t d)")
                        e.tensor_tensor(mine, mine, cs[:, bass.ds((b + 1) & 1, 1), :, :].rearrange("p a t d -> p (a t d)"),
                                        ALU.add)
                    e.drain().then_inc(summed, 1)

            def after(t):
                e.drain()
                norm = k.norm[:, bass.ds(t, 1)]
                if first:
                    count = agg[:, 2 * D:]
                    e.tensor_scalar(small[:, 0, :], count, 1.0, None, ALU.max)
                    e.scalar_tensor_tensor(small[:, 1, :], count, 0.0, k.rank8[:, :], ALU.is_gt, ALU.mult)
                    e.tensor_copy(k.attr[:, bass.ds(t, 1), :].rearrange("p a f -> p (a f)"), agg[:, D:2 * D])
                    e.drain()
                    e.reciprocal(small[:, 2, :], small[:, 0, :])
                    e.reduce_max(best[:, :], small[:, 1, :], AX.X)
                    e.drain()
                    e.scalar_tensor_tensor(small[:, 3, :], count, 0.0, small[:, 2, :], ALU.is_gt, ALU.mult)
                    e.drain()
                    e.scalar_tensor_tensor(small[:, 2, :], small[:, 1, :], best[:, 0:1], small[:, 3, :],
                                           ALU.is_equal, ALU.mult)
                    e.drain()
                    e.reduce_sum(norm, small[:, 2, :], AX.X)
                    e.drain()
                    e.wait_ge(ht_ps, t)
                e.scalar_tensor_tensor(h[:, :], agg[:, 0:D], norm, k.self_[:, bass.ds(t, 1), :].rearrange("p a f -> p (a f)"),
                                       ALU.mult, ALU.add)
                e.drain()
                e.tensor_tensor(h[:, :], h[:, :], k.bns[:, l, :], ALU.mult)
                e.drain()
                e.tensor_tensor(h[:, :], h[:, :], k.bnb[:, l, :], ALU.add)
                e.drain()
                if first:
                    e.tensor_scalar(h[:, :], h[:, :], 0.0, None, ALU.max).then_inc(h_made, 1)
                    return
                x = k.x[:, bass.ds(t, 1), :].rearrange("p a f -> p (a f)")
                e.scalar_tensor_tensor(x, h[:, :], 0.0, x, ALU.max, ALU.add)
                e.drain()
                tile_stats(e, k, x, t)

            rounds(e, body, before, after)
            if not first:
                normalize(e, k, 1)


def tile_stats(e, k, x, t):
    e.bn_stats(k.stat[:, :], x)
    e.drain()
    e.bn_aggr(k.mv1[:, :], k.stat[:, :])
    e.drain()
    e.tensor_copy(k.mv[:, bass.ds(t, 1), :].rearrange("p a c -> p (a c)"), k.mv1[:, :])


def roots(e, k, nth):
    e.wait_ge(k.vars_made, nth)
    e.activation(k.rstd[:, :], k.mv[:, :, 1], ACT.Sqrt, bias=k.lneps[:, 0:1]).then_inc(k.roots_made, 1)


def normalize(e, k, nth, made=None, rows=None):
    e.drain().then_inc(k.vars_made, 1)
    e.wait_ge(k.roots_made, nth)
    e.reciprocal(k.rstd[:, :], k.rstd[:, :])
    e.drain()
    with e.Fori(0, NT) as t:
        x = (k.x if rows is None else rows)[:, bass.ds(t, 1), :].rearrange("p a f -> p (a f)")
        m = e.tensor_scalar(x, x, k.mv[:, bass.ds(t, 1), 0], k.rstd[:, bass.ds(t, 1)], ALU.subtract, ALU.mult)
        if made:
            m.then_inc(made, 1)


def phase_sum_to_source(nc, k):
    with ExitStack() as ctx:
        sb = lambda name, shape, dt=F32: ctx.enter_context(nc.sbuf_tensor("s_" + name, shape, dt))
        sem = lambda name: ctx.enter_context(nc.semaphore("s_" + name))
        ring = sb("ring", [P, SEG, HALF])
        xl = sb("xl", [P, SEG, D])
        acc = ctx.enter_context(nc.psum_tensor("s_acc", [P, 8, 512], F32))
        total = k.self_[:, :, :].rearrange("p t f -> p (t f)")
        rows_in = [sem(f"rows_in{i}") for i in range(SEG)]
        xl_made, used, emptied, turned, taken = sem("xl_made"), sem("used"), sem("emptied"), sem("turned"), sem("taken")
        block = ctx.enter_context(nc.Block())

        @block.sync
        def _(e):
            for h in range(2):
                with e.Fori(0, NSEG) as tb:
                    for i in range(SEG):
                        e.wait_ge(used, tb * SEG + (h * NT + i + 1))
                        e.dma_start(ring[:, i, :], k.cd_d[bass.ds(tb * SEG + i, 1), :, h * HALF:(h + 1) * HALF]
                                    .rearrange("a p c -> (a p) c")).then_inc(rows_in[i], 16)

        @block.gpsimd
        def _(e):
            for h in range(2):
                with e.Fori(0, NSEG) as tb:
                    for i in range(SEG):
                        e.wait_ge(used, tb * SEG + (h * NT + i + 1))
                        e.tensor_copy(xl[:, i, :], k.x[:, bass.ds(tb * SEG + i, 1), :].rearrange("p a f -> p (a f)"))\
                         .then_inc(xl_made, 1)

        @block.tensor
        def _(e):
            e.sem_inc(used, SEG)

            def batch(h, tb, start, stop):
                for i in range(SEG):
                    e.wait_ge(rows_in[i], (tb + (h * NSEG + 1)) * 16)
                    e.wait_ge(xl_made, tb * SEG + (h * NT + i + 1))
                    for s in range(NSEG):
                        m = e.matmul(acc[:, s, 0:HSEG], xl[:, i, :], ring[:, i, s * HSEG:(s + 1) * HSEG],
                                     start=start and i == 0, stop=stop and i == SEG - 1)
                    m.then_inc(used, 1)

            for h in range(2):
                if h:
                    e.wait_ge(emptied, NSEG)
                batch(h, 0, True, False)
                with e.Fori(1, NSEG - 1) as tb:
                    batch(h, tb, False, False)
                batch(h, NSEG - 1, False, True)
            e.wait_ge(emptied, 2 * NSEG)
            for t in range(NT):
                if t >= 2 * SEG and t % SEG == 0:
                    e.wait_ge(taken, t // SEG - 1)
                b = t // SEG % 2
                m = e.transpose(acc[:, 2 * b:2 * b + 2, :].rearrange("p a c -> p (a c)")[:, t % SEG * P:(t % SEG + 1) * P],
                                total[:, t * P:(t + 1) * P], k.ident[:, :])
                if t % SEG == SEG - 1:
                    m.then_inc(turned, 1)

        @block.scalar
        def _(e):
            for h in range(2):
                e.wait_ge(used, SEG + (h + 1) * NT)
                for s in range(NSEG // 2, NSEG):
                    e.activation(total[:, h * HALF + s * HSEG:h * HALF + (s + 1) * HSEG], acc[:, s, 0:HSEG], ACT.Copy)\
                     .then_inc(emptied, 1)
            roots(e, k, 2)

        @block.vector
        def _(e):
            for h in range(2):
                e.wait_ge(used, SEG + (h + 1) * NT)
                for s in range(NSEG // 2):
                    e.tensor_copy(total[:, h * HALF + s * HSEG:h * HALF + (s + 1) * HSEG], acc[:, s, 0:HSEG])\
                     .then_inc(emptied, 1)
            with e.Fori(0, NSEG) as tb:
                e.wait_ge(turned, tb + 1)
                x = k.x[:, bass.ts(tb, SEG), :].rearrange("p a f -> p (a f)")
                e.scalar_tensor_tensor(x, x, 2.0, acc[:, bass.ds((tb & 1) * 2, 2), :].rearrange("p a c -> p (a c)")[:, 0:SW],
                                       ALU.mult, ALU.add).then_inc(taken, 1)
                e.drain()
                batch_stats(e, k, k.x, tb)
            normalize(e, k, 2)


def batch_stats(e, k, x, tb):
    for i in range(SEG):
        e.bn_stats(k.stat7[:, i, :], x[:, bass.ds(tb * SEG + i, 1), :].rearrange("p a f -> p (a f)"))
    e.drain()
    for i in range(SEG):
        e.bn_aggr(k.mv7[:, i, :], k.stat7[:, i, :])
    e.drain()
    e.tensor_copy(k.mv[:, bass.ts(tb, SEG), :], k.mv7[:, :, :])
    e.drain()


def phase_attention(nc, k):
    with ExitStack() as ctx:
        sb = lambda name, shape, dt=F32: ctx.enter_context(nc.sbuf_tensor("a_" + name, shape, dt))
        pb = lambda name, shape, dt=F32: ctx.enter_context(nc.psum_tensor("a_" + name, shape, dt))
        sem = lambda name: ctx.enter_context(nc.semaphore("a_" + name))
        wide = 2 * D + 2
        wmsg = sb("wmsg", [P, D])
        attn = sb("attn", [P, 2])
        wcat = sb("wcat", [P, wide])
        wfrom = sb("wfrom", [P, P])
        coef = sb("coef", [P, 1])
        sig = sb("sig", [P, 1])
        score = sb("score", [P, 2, NT])
        leaky_from = sb("leaky_from", [P, NT])
        frow = k.self_[:, :, :].rearrange("p t f -> p (t f)")
        pen = sb("pen", [P, 2, NPAD], BF16)
        best = sb("best", [P, SEG])
        t7 = sb("t7", [P, 4, SEG])
        diag = sb("diag", [P, 2, SEG, P])
        ones = sb("ones", [P, P])
        counts = sb("counts", [P, 2, SEG, SW])
        powers = sb("powers", [P, 2, 2, SW])
        xs, xt = powers[:, 0, 0, :], powers[:, 0, 1, :]
        weights = sb("weights", [P, SEG, SW])
        den = sb("den", [P, SEG])
        fresh = sb("fresh", [P, SEG, D])
        weights_in, wcat_ps, wcat_made, consts = sem("weights_in"), sem("wcat_ps"), sem("wcat_made"), sem("consts")
        coef_exp, sig_made = sem("coef_exp"), sem("sig_made")
        xs_made, xt_ps, xt_sb = sem("xs_made"), sem("xt_ps"), sem("xt_sb")
        msg_ps, msg_act, msg_dve, frow_ps, frow_sb = sem("msg_ps"), sem("msg_act"), sem("msg_dve"), sem("frow_ps"), sem("frow_sb")
        pen_in = [sem(f"pen_in{i}") for i in range(2)]
        counts_in = [sem(f"counts_in{i}") for i in range(2)]
        pen_used, diag_made, uv_made = sem("pen_used"), sem("diag_made"), sem("uv_made")
        powered, weighed, summed, counts_free, closed = sem("powered"), sem("weighed"), sem("summed"), sem("counts_free"), sem("closed")

        powered_free, turn, dve_turn = sem("powered_free"), sem("turn"), sem("dve_turn")
        psum = pb("psum", [P, 8, 512])
        bank2 = lambda i: psum[:, i:i + 2, :].rearrange("p a c -> p (a c)")
        block = ctx.enter_context(nc.Block())

        @block.sync
        def _(e):
            for t, ap in ((wmsg[:, :], k.ins["w_msg"]),
                          (attn[:, :], k.ins["attn_w"].rearrange("(c p) -> p c", c=2)),
                          (wcat[:, 0:D], k.ins["w_msg_transposed"]),
                          (wcat[:, D + 2:], k.ins["w_res_transposed"]),
                          (coef[:, :], k.ins["coef"].partition_broadcast(P))):
                e.dma_start(t, ap, allow_slow_non_contiguous=True).then_inc(weights_in, 16)
            with e.Fori(0, NSEG) as tg:
                for i in range(SEG):
                    e.wait_ge(pen_used, tg * SEG + max(0, i - 1))
                    e.dma_start(pen[:, i % 2, :], k.pen_d[bass.ds(tg * SEG + i, 1), :, :].rearrange("a p c -> (a p) c"))\
                     .then_inc(pen_in[i % 2], 16)
                for hb in range(NSEG):
                    e.wait_ge(counts_free, tg * NSEG + max(0, hb - 1))
                    e.sem_inc(turn, 1)
                    e.dma_start(counts[:, hb % 2, :, :], k.cs_d[bass.ts(tg, SEG), :, hb * SW:(hb + 1) * SW]
                                .rearrange("t p c -> p t c")).then_inc(counts_in[hb % 2], 16)

        @block.gpsimd
        def _(e):
            e.memset(ones[:, :], 1.0).then_inc(consts, 1)
            e.memset(k.msg[:, :, D:D + 1], 1.0).then_inc(consts, 1)
            with e.Fori(0, NSEG) as tb:
                e.wait_ge(xt_ps, tb)
                e.tensor_copy(xs, k.x[:, bass.ts(tb, SEG), :].rearrange("p a f -> p (a f)")).then_inc(xs_made, 1)

        @block.tensor
        def _(e):
            e.wait_ge(weights_in, 5 * 16)
            e.matmul(psum[:, 0, 0:2], wmsg[:, :], attn[:, :], start=True, stop=True).then_inc(wcat_ps, 1)
            e.wait_ge(wcat_made, 1)
            with e.Fori(0, NSEG) as tb:
                e.wait_ge(xs_made, tb + 1)
                e.wait_ge(xt_sb, tb)
                for i in range(SEG):
                    m = e.transpose(bank2(0)[:, i * P:(i + 1) * P], xs[:, i * P:(i + 1) * P], k.ident[:, :])
                m.then_inc(xt_ps, 1)
                e.wait_ge(xt_sb, tb + 1)
                e.wait_ge(frow_sb, tb)
                for s in range(2):
                    m = e.matmul(psum[:, 2 + s, 0:SW // 2], wfrom[:, :], xt[:, s * SW // 2:(s + 1) * SW // 2],
                                 start=True, stop=True)
                m.then_inc(frow_ps, 1)
                for i in range(SEG):
                    e.wait_ge(msg_dve, tb * SEG + max(0, i - 3))
                    e.matmul(psum[:, 4 + i % 4, 0:wide], xt[:, i * P:(i + 1) * P], wcat[:, :], start=True, stop=True)\
                     .then_inc(msg_ps, 1)
            e.wait_ge(consts, 2)
            e.wait_ge(frow_sb, NSEG)
            e.wait_ge(msg_act, NT)
            e.wait_ge(msg_dve, NT)
            with e.Fori(0, NSEG) as tg:
                e.wait_ge(diag_made, tg + 1)
                for v in range(2):
                    d = diag[:, v, :, :].rearrange("p a c -> p (a c)")
                    for c0, c1 in ((0, 512), (512, SW)):
                        m = e.matmul(bank2(2 * v)[:, c0:c1], ones[:, :], d[:, c0:c1], start=True, stop=True)
                m.then_inc(uv_made, 1)
                e.wait_ge(closed, tg)
                for first, lo, hi in ((True, 0, 1), (False, 1, NSEG)):
                    with ExitStack() as loop:
                        hb = 0 if first else loop.enter_context(e.Fori(lo, hi))
                        for j in range(SEG):
                            n = tg * NT + hb * SEG + j
                            e.wait_ge(weighed, n + 1)
                            for i in range(SEG):
                                m = e.matmul(psum[:, 4 + i // 3, i % 3 * (D + 4):i % 3 * (D + 4) + D + 1],
                                             weights[:, j, i * P:(i + 1) * P],
                                             k.msg[:, bass.ds(hb * SEG + j, 1), :].rearrange("p a f -> p (a f)"),
                                             start=first and j == 0 and i % 3 == 0, stop=j == SEG - 1,
                                             skip_group_check=True)
                            m.then_inc(summed, 1)

        @block.scalar
        def _(e):
            e.wait_ge(weights_in, 5 * 16)
            e.activation(sig[:, :], coef[:, :], ACT.Exp, scale=-1.0).then_inc(coef_exp, 1)
            with e.Fori(0, NSEG) as tb:
                e.wait_ge(xt_ps, tb + 1)
                e.wait_ge(msg_ps, tb * SEG)
                e.activation(xt, bank2(0)[:, 0:SW], ACT.Copy).then_inc(xt_sb, 1)
                e.wait_ge(frow_ps, tb + 1)
                e.activation(frow[:, bass.ts(tb, SW)].rearrange("p (s c) -> p s c", s=2), psum[:, 2:4, 0:SW // 2], ACT.Copy)\
                 .then_inc(frow_sb, 1)
                for i in range(SEG):
                    e.wait_ge(msg_ps, tb * SEG + (i + 1))
                    e.activation(k.msg[:, bass.ds(tb * SEG + i, 1), 0:D].rearrange("p a f -> p (a f)"),
                                 psum[:, 4 + i % 4, 0:D], ACT.Copy).then_inc(msg_act, 1)
            e.wait_ge(msg_dve, NT)
            e.activation(leaky_from[:, :], score[:, 0, :], ACT.Copy, scale=LEAKY).then_inc(sig_made, 1)
            e.wait_ge(sig_made, 1)
            with e.Fori(0, NSEG) as tg:
                e.wait_ge(uv_made, tg + 1)
                with e.Fori(0, NSEG) as hb:
                    for j in range(SEG):
                        n = hb * SEG + j
                        total = tg * NT + n
                        e.wait_ge(powered_free, total + 1)
                        for v, f in ((0, score[:, 0, bass.ds(n, 1)]), (1, leaky_from[:, bass.ds(n, 1)])):
                            m = e.activation(powers[:, bass.ds(total & 1, 1), v, :].rearrange("p a c -> p (a c)"),
                                             bank2(2 * v)[:, 0:SW], ACT.Exp, bias=f)
                        m.then_inc(powered, 1)
            roots(e, k, 3)

        @block.vector
        def _(e):
            e.sem_inc(powered_free, 2)
            e.wait_ge(wcat_ps, 1)
            e.tensor_copy(wcat[:, D:D + 2], psum[:, 0, 0:2])
            e.wait_ge(coef_exp, 1)
            e.tensor_scalar(sig[:, :], sig[:, :], 1.0, None, ALU.add)
            e.drain()
            e.tensor_copy(wfrom[:, :], wcat[:, D:D + 1].to_broadcast([P, P]))
            e.reciprocal(sig[:, :], sig[:, :])
            e.drain().then_inc(wcat_made, 1)
            with e.Fori(0, NSEG) as tb:
                e.wait_ge(xs_made, tb + 1)
                for i in range(SEG):
                    t = tb * SEG + i
                    e.wait_ge(msg_act, t + 1)
                    e.tensor_copy(score[:, :, bass.ds(t, 1)].rearrange("p a b -> p (a b)"), psum[:, 4 + i % 4, D:D + 2])
                    x = k.x[:, bass.ds(t, 1), :].rearrange("p a f -> p (a f)")
                    e.scalar_tensor_tensor(x, psum[:, 4 + i % 4, D + 2:wide], sig[:, 0:1], x, ALU.mult, ALU.add)
                    e.drain().then_inc(msg_dve, 1)
            e.wait_ge(frow_sb, NSEG)
            e.wait_ge(consts, 2)
            with e.Fori(0, NSEG) as tg:
                for i in range(SEG):
                    w = i % 2
                    e.wait_ge(pen_in[w], (tg * (4 - w) + (i // 2 + 1)) * 16)
                    if i == 0:
                        e.wait_ge(summed, tg * NT)
                    e.sem_inc(dve_turn, 1)
                    e.tensor_tensor_reduce(out=weights[:, :, :].rearrange("p a c -> p (a c)"), in0=pen[:, w, :], in1=frow,
                                           scale=1.0, scalar=FAR, op0=ALU.add, op1=ALU.max, accum_out=best[:, i:i + 1])
                    e.drain().then_inc(pen_used, 1)
                e.scalar_tensor_tensor(best[:, :], best[:, :], FAR / 2, best[:, :], ALU.is_gt, ALU.mult)
                e.tensor_copy(t7[:, 0, :], score[:, 1, bass.ts(tg, SEG)])
                e.drain()
                e.tensor_tensor(t7[:, 1, :], t7[:, 0, :], best[:, :], ALU.add)
                e.drain()
                e.scalar_tensor_tensor(t7[:, 1, :], t7[:, 1, :], LEAKY, t7[:, 1, :], ALU.mult, ALU.max)
                e.drain()
                e.tensor_tensor(t7[:, 2, :], t7[:, 0, :], t7[:, 1, :], ALU.subtract)
                e.scalar_tensor_tensor(t7[:, 3, :], t7[:, 0, :], LEAKY, t7[:, 1, :], ALU.mult, ALU.subtract)
                e.drain()
                for v in range(2):
                    for i in range(SEG):
                        m = e.tensor_scalar(diag[:, v, i, :], k.ident[:, :], t7[:, 2 + v, i:i + 1], None, ALU.mult)
                m.then_inc(diag_made, 1)
                for hb in range(NSEG):
                    e.wait_ge(counts_in[hb % 2], (tg * (4 - hb % 2) + (hb // 2 + 1)) * 16)
                    for j in range(SEG):
                        n = tg * NT + (hb * SEG + j)
                        e.wait_ge(powered, n + 1)
                        if hb or j:
                            e.wait_ge(summed, tg * NT + max(0, hb * SEG + j - SEG + 1))
                        p = [powers[:, bass.ds(n & 1, 1), v, :].rearrange("p a c -> p (a c)") for v in range(2)]
                        e.tensor_tensor(p[0], p[0], p[1], ALU.max)
                        e.drain()
                        e.scalar_tensor_tensor(weights[:, j, :].rearrange("p (i c) -> p i c", c=P),
                                               p[0].rearrange("p (i c) -> p i c", c=P), 1.0,
                                               counts[:, hb % 2, :, j * P:(j + 1) * P], ALU.min, ALU.mult)
                        e.drain().then_inc(weighed, 1)
                        e.sem_inc(powered_free, 1)
                    e.sem_inc(counts_free, 1)
                e.wait_ge(summed, (tg + 1) * NT)
                for i in range(SEG):
                    e.tensor_scalar(den[:, i:i + 1], psum[:, 4 + i // 3, i % 3 * (D + 4) + D:i % 3 * (D + 4) + D + 1],
                                    1e-30, None, ALU.max)
                e.drain()
                e.reciprocal(den[:, :], den[:, :])
                e.drain()
                for i in range(SEG):
                    e.tensor_scalar(fresh[:, i, :], psum[:, 4 + i // 3, i % 3 * (D + 4):i % 3 * (D + 4) + D],
                                    den[:, i:i + 1], 0.0, ALU.mult, ALU.max)
                e.drain().then_inc(closed, 1)
                x = k.x[:, bass.ts(tg, SEG), :]
                e.tensor_tensor(x, x, fresh[:, :, :], ALU.add)
                e.drain()
                batch_stats(e, k, k.x, tg)
            normalize(e, k, 3)


def phase_edge_sum(nc, k):
    with ExitStack() as ctx:
        sb = lambda name, shape, dt=F32: ctx.enter_context(nc.sbuf_tensor("e_" + name, shape, dt))
        sem = lambda name: ctx.enter_context(nc.semaphore("e_" + name))
        ring = sb("ring", [P, NSEG, SW])
        attr = sb("attr", [P, NT, D])
        y = k.self_
        acc = ctx.enter_context(nc.psum_tensor("e_acc", [P, 2, 512], F32))
        seg_in = [sem(f"seg_in{g}") for g in range(NSEG)]
        attr_in, used, taken = sem("attr_in"), sem("used"), sem("taken")
        made, stored = sem("made"), sem("stored")
        block = ctx.enter_context(nc.Block())

        @block.sync
        def _(e):
            e.dma_start(attr[:, :, :].rearrange("p t f -> p (t f)"), k.attr_d).then_inc(attr_in, 16)
            with e.Fori(0, NT) as t:
                for g in range(NSEG):
                    e.wait_ge(used, t * NSEG + (g + 1))
                    e.dma_start(ring[:, g, :], k.cs_d[bass.ds(t, 1), :, g * SW:(g + 1) * SW].rearrange("a p c -> (a p) c"))\
                     .then_inc(seg_in[g], 16)
            e.wait_ge(made, NT)
            full = NT - 1
            e.dma_start(k.out[0:full * P, :].rearrange("(t p) f -> p t f", p=P), y[:, 0:full, :]).then_inc(stored, 16)
            e.dma_start(k.out[full * P:NODES, :], y[0:LAST, full, :]).then_inc(stored, 16)
            e.wait_ge(stored, 32)

        @block.tensor
        def _(e):
            e.sem_inc(used, NSEG)
            with e.Fori(0, NT) as t:
                e.wait_ge(taken, t + 1)
                for g in range(NSEG):
                    e.wait_ge(seg_in[g], (t + 1) * 16)
                    for i in range(SEG):
                        m = e.matmul(acc[:, bass.ds(t & 1, 1), 0:D].rearrange("p a f -> p (a f)"),
                                     ring[:, g, i * P:(i + 1) * P], k.x[:, g * SEG + i, :],
                                     start=g == 0 and i == 0, stop=g == NSEG - 1 and i == SEG - 1)
                    m.then_inc(used, 1)

        @block.scalar
        def _(e):
            roots(e, k, 4)

        @block.vector
        def _(e):
            e.sem_inc(taken, 2)
            e.wait_ge(attr_in, 16)
            with e.Fori(0, NT) as t:
                row = lambda a: a[:, bass.ds(t, 1), :].rearrange("p a f -> p (a f)")
                e.tensor_tensor(row(y), row(k.x), row(attr), ALU.add)
                e.drain()
                e.wait_ge(used, t * NSEG + 2 * NSEG)
                e.tensor_tensor(row(y), row(y), acc[:, bass.ds(t & 1, 1), 0:D].rearrange("p a f -> p (a f)"), ALU.add)
                e.drain().then_inc(taken, 1)
                tile_stats(e, k, row(y), t)
            normalize(e, k, 4, made, y)


def layout(inputs):
    import numpy as np

    a = {n: np.asarray(v) for n, v in inputs.items()}
    edges = EPAD - EDGES
    got = {n: v for n, v in a.items() if n.startswith("L0")}
    got["x"] = np.pad(a["x"], ((0, NPAD - NODES), (0, 0)))
    got["x_transposed"] = np.ascontiguousarray(got["x"].T)
    got["src"] = np.pad(a["src"], (0, edges))
    got["dst"] = np.pad(a["dst"], (0, edges), constant_values=PAD_DST)
    got["edge_type_8"] = np.pad(a["edge_type_8"], (0, edges))
    got["edge_attr_128"] = np.pad(a["edge_attr_128"], ((0, edges), (0, 0)))
    got["w_msg"] = a["L2_gnn_W_msg"]
    got["w_msg_transposed"] = np.ascontiguousarray(a["L2_gnn_W_msg"].T)
    got["w_res_transposed"] = np.ascontiguousarray(a["L2_gnn_W_res"].T)
    got["attn_w"] = a["L2_gnn_attn_w"]
    got["coef"] = a["L2_gnn_passthrough_coef"]
    return got


def kernel(**inputs):
    import numpy as np
    import concourse.bacc as bacc
    from concourse.bass_utils import run_bass_kernel_spmd

    nc = bacc.Bacc("TRN2", target_bir_lowering=False, num_devices=1)
    arrays = {f"in_{n}": v for n, v in layout(inputs).items()}
    ins = {n[3:]: nc.dram_tensor(n, v.shape, mybir.dt.from_np(v.dtype), kind="ExternalInput").ap()
           for n, v in arrays.items()}
    out = nc.dram_tensor("out", (NODES, D), F32, kind="ExternalOutput").ap()
    build(nc, ins, out)
    return run_bass_kernel_spmd(nc, [arrays], core_ids=[0]).results[0]["out"]
```

```python
from contextlib import ExitStack

import concourse.bass as bass
from concourse import mybir

ALU = mybir.AluOpType
ACT = mybir.ActivationFunctionType
AX = mybir.AxisListType
F32 = mybir.dt.float32
F16 = mybir.dt.float16
BF16 = mybir.dt.bfloat16
I32 = mybir.dt.int32

P = 128
D = 128
NODES, EDGES = 6250, 206250
RELATIONS, BASES, LAYERS = 8, 4, 2
BN_EPS, LN_EPS, LEAKY = 1e-3, 1e-5, 0.01

NT = -(-NODES // P)
NPAD = NT * P
LAST = NODES - (NT - 1) * P
CHUNK = 64
EPP = 1664
EPAD = P * EPP
CPP = EPP // CHUNK
CHUNKS = EPAD // CHUNK
REAL_CHUNKS = -(-EDGES // CHUNK)
PAD_DST = 8192

GROUPS, PER = 7, 5
SLOTS = GROUPS * PER
TILE_STEP = SLOTS * P // CHUNK
WIN = 8
NW = NPAD // WIN
WPT = P // WIN
WSLOTS = 3
WIN_STEP = WSLOTS * P // CHUNK
WGROUPS = 7
WPG = NW // WGROUPS
REC = 5
TW = RELATIONS * D
GW = 2 * D + RELATIONS
WC = NT * WIN
SEG = 7
SW = SEG * P
NSEG = NT // SEG
HALF = NSEG * SW // 2
HSEG = HALF // NSEG
EXACT = 2048
NARROW_SPAN = EXACT // CHUNK * TILE_STEP
SCALE = 4096.0
ON_POOL = (0, 1, 3, 4, 6)
LAG = 2
FAR = -3.0e38

assert NT == SEG * NSEG and EPAD - REAL_CHUNKS * CHUNK >= SLOTS * P


class Kernel:
    pass


def spread(ap, n):
    return ap.unsqueeze(len(ap.shape)).to_broadcast([*ap.shape, n])


def cells(ap, wide):
    return ap if wide else ap.bitcast(F16)[:, 0:ap.shape[1]]


def either(e, k, program):
    with e.If(e.value_load(k.most[0:1, 0:1], min_val=1, max_val=CHUNKS * TILE_STEP) > NARROW_SPAN):
        program(True)
    with e.Else():
        program(False)


def split_rows(e, x, parts, rest, tb, made):
    x = x[:, bass.ts(tb, SEG), :]
    part = [parts[:, bass.ts(tb, SEG), i * D:(i + 1) * D] for i in range(2)]
    e.tensor_scalar(part[0], x, SCALE, None, ALU.mult)
    e.drain()
    e.scalar_tensor_tensor(rest, x, SCALE, part[0], ALU.mult, ALU.subtract)
    e.drain()
    e.tensor_copy(part[1], rest)
    e.drain().then_inc(made, 1)


def repeat(ap, n):
    return ap.unsqueeze(1).to_broadcast([ap.shape[0], n, ap.shape[1]])


def build(nc, ins, out):
    k = Kernel()
    dram = lambda name, shape, dt=F32: nc.dram_tensor(name, shape, dt, kind="Internal").ap()
    k.rec_d = dram("edge_records", (EPAD * REC,))
    k.chunk_d = dram("chunk_bounds", (2, CHUNKS))
    k.wspan_d = dram("window_spans", (NW,))
    k.wlo_d = dram("window_starts", (NW,), I32)
    k.tile_d = dram("tile_starts_and_spans", (2, NT), I32)
    k.table_d = [dram(f"table_{l}", (NPAD * RELATIONS, D)) for l in range(LAYERS)]
    k.cs_d = {w: dram("counts_by_source_" + n, (NT, P, NPAD), t) for w, n, t in ((True, "f32", F32), (False, "f16", F16))}
    k.cd_d = {w: dram("counts_by_destination_" + n, (NT, P, NPAD), t) for w, n, t in ((True, "f32", F32), (False, "f16", F16))}
    k.pen_d = dram("no_edge_penalty", (NT, P, NPAD), BF16)
    k.attr_d = dram("attribute_sums", (P, NPAD))
    k.ins, k.out = ins, out
    with ExitStack() as ctx:
        sb = lambda name, shape, dt=F32: ctx.enter_context(nc.sbuf_tensor(name, shape, dt))
        k.vars_made = ctx.enter_context(nc.semaphore("variances_made"))
        k.roots_made = ctx.enter_context(nc.semaphore("roots_made"))
        both = sb("state_and_spare", [P, 2 * NPAD + NT])
        k.pair = both[:, 0:2 * NPAD].rearrange("p (a t f) -> p a t f", a=2, f=D)
        k.x, k.spare = k.pair[:, 0], k.pair[:, 1]
        k.msg = both[:, NPAD:].rearrange("p (t f) -> p t f", f=D + 1)
        k.self_ = sb("self_term", [P, NT, D])
        k.ident = sb("ident", [P, P])
        k.ident16 = sb("ident16", [P, P], F16)
        k.most = sb("greatest_span", [1, 1], I32)
        k.lneps = sb("ln_eps", [P, 1])
        k.stat = sb("stat", [P, 6])
        k.stat7 = sb("stat_of_seven", [P, SEG, 6])
        k.mv7 = sb("mean_var_of_seven", [P, SEG, 2])
        k.mv1 = sb("mean_var_of_tile", [P, 2])
        k.mv = sb("mean_var", [P, NT, 2])
        k.rstd = sb("rstd", [P, NT])
        with ExitStack() as layers:
            inner = lambda name, shape, dt=F32: layers.enter_context(nc.sbuf_tensor(name, shape, dt))
            k.attr = inner("attr_sum", [P, NT, D])
            k.rank8 = inner("rank8", [P, RELATIONS])
            k.iota8 = inner("iota8", [P, RELATIONS])
            k.iota16 = inner("iota16", [P, WC], F16)
            k.iota = inner("iota", [P, P])
            k.wbase = inner("window_base", [P, NT, WPT])
            k.tbase = inner("minus_tile_base", [P, NT])
            k.wr = inner("relation_weights", [P, LAYERS, TW])
            k.loop = inner("loop_weights", [P, LAYERS, D])
            k.bns = inner("bn_scale", [P, LAYERS, D])
            k.bnb = inner("bn_shift", [P, LAYERS, D])
            k.norm = inner("norm", [P, NT])
            k.tlo = inner("tile_start_row", [1, NT], I32)
            k.tspan = inner("tile_span_row", [1, NT], I32)
            k.wlo = inner("window_start_row", [1, NW], I32)
            phase_prepare(nc, k)
            phase_layer(nc, k, 0)
            phase_layer(nc, k, 1)
        phase_sum_to_source(nc, k)
        phase_attention(nc, k)
        phase_edge_sum(nc, k)


def phase_prepare(nc, k):
    with ExitStack() as ctx:
        sb = lambda name, shape, dt=F32: ctx.enter_context(nc.sbuf_tensor(name, shape, dt))
        sem = lambda name: ctx.enter_context(nc.semaphore("p_" + name))
        a = k.ins
        work = sb("work", [P, 5 * CHUNKS])
        src, dst, typ, itmp = (work[:, i * EPP:(i + 1) * EPP].bitcast(I32) for i in range(4))
        dstf = work[:, 4 * EPP:5 * EPP]
        rec = work[:, 5 * EPP:(5 + REC) * EPP].rearrange("p (e w) -> p e w", w=REC)
        bounds = work[:, 0:2 * CHUNKS].rearrange("p (m c) -> p m c", m=2)
        scr = work[:, 2 * CHUNKS:4 * CHUNKS].rearrange("p (m c) -> p m c", m=2)
        asc = work[:, 4 * CHUNKS:5 * CHUNKS]
        desc = k.attr[:, :, :].rearrange("p t f -> p (t f)")[:, 0:CHUNKS]
        cm = sb("chunk_min_max", [P, 2, CPP])
        lob = sb("lob", [P, WGROUPS + 1])
        hib = sb("hib", [P, WGROUPS + 1])
        m1 = sb("m1", [P, WGROUPS + 1])
        m2 = sb("m2", [P, WGROUPS + 1])
        wsp = sb("wsp", [P, WGROUPS + 1])
        loi = sb("loi", [P, WGROUPS + 1], I32)
        wt = sb("wt", [NT, WPT])
        smax = sb("smax", [NT, 1])
        smaxf = sb("smaxf", [NT, 1])
        smaxi = sb("smaxi", [NT, 1], I32)
        spanf = sb("spanf", [1, NT])
        mostf = sb("mostf", [1, 1])
        wemb = sb("wemb", [P, D])
        bemb = sb("bemb", [P, 1])
        bases = sb("bases", [P, LAYERS, BASES, D])
        coe = sb("coe", [P, LAYERS * RELATIONS * BASES])
        bn = [sb(f"bn{i}", [P, LAYERS, D]) for i in range(4)]
        eps = sb("eps", [P, 1])
        identz = sb("identz", [P, P])
        xt = k.x[:, :, :].rearrange("p t f -> p (t f)")
        ht = sb("ht", [P, SW])
        TSLOTS = 3
        tsb = k.spare.rearrange("p t f -> p (t f)")[:, 0:TSLOTS * TW].rearrange("p (s w) -> p s w", s=TSLOTS)
        ph = ctx.enter_context(nc.psum_tensor("ph", [P, 1024], F32))
        pt = ctx.enter_context(nc.psum_tensor("pt", [P, 2, 1024], F32))
        pse = ctx.enter_context(nc.psum_tensor("pse", [P, 2, 512], F32))

        edges_in, weights_in, x_in = sem("edges_in"), sem("weights_in"), sem("x_in")
        CONSTS = 16
        consts, rec_made, rec_out = sem("consts"), sem("rec_made"), sem("rec_out")
        chunk_out, bounds_in = sem("chunk_out"), sem("bounds_in")
        spans_made, spans_out, spans_in = sem("spans_made"), sem("spans_out"), sem("spans_in")
        tiles_made, tiles_out, rows_in = sem("tiles_made"), sem("tiles_out"), sem("rows_in")
        wr_made, var_made = sem("wr_made"), sem("var_made")
        ht_ps, ht_sb, t_ps, t_bank = sem("ht_ps"), sem("ht_sb"), sem("t_ps"), sem("t_bank")
        t_out = [sem(f"t_out{i}") for i in range(TSLOTS)]
        block = ctx.enter_context(nc.Block())

        @block.sync
        def _(e):
            for t, name in ((dst, "dst"), (src, "src"), (typ, "edge_type_8")):
                e.dma_start(t, a[name].rearrange("(p c) -> p c", p=P)).then_inc(edges_in, 16)
            e.dma_start(xt, a["x_transposed"]).then_inc(x_in, 16)
            e.wait_ge(rec_made, 1)
            e.dma_start(k.chunk_d.rearrange("m (p c) -> p m c", p=P), cm[:, :, :]).then_inc(chunk_out, 16)
            e.wait_ge(rec_made, 2)
            e.dma_start(k.rec_d.rearrange("(p c) -> p c", p=P), work[:, 5 * EPP:(5 + REC) * EPP]).then_inc(rec_out, 16)
            e.wait_ge(chunk_out, 16)
            e.dma_start(work[:, 0:2 * CHUNKS], k.chunk_d.rearrange("m c -> (m c)").partition_broadcast(P))\
             .then_inc(bounds_in, 16)
            e.wait_ge(spans_made, 1)
            e.dma_start(k.wspan_d.rearrange("(g p) -> p g", p=WPG), wsp[0:WPG, 0:WGROUPS],
                        allow_slow_non_contiguous=True).then_inc(spans_out, 16)
            e.dma_start(k.wlo_d.rearrange("(g p) -> p g", p=WPG), loi[0:WPG, 0:WGROUPS],
                        allow_slow_non_contiguous=True).then_inc(spans_out, 16)
            e.wait_ge(spans_out, 32)
            e.dma_start(wt[:, :], k.wspan_d.rearrange("(t q) -> t q", q=WPT)).then_inc(spans_in, 16)
            e.dma_start(k.wlo[:, :], k.wlo_d.rearrange("(a w) -> a w", a=1)).then_inc(rows_in, 16)
            e.wait_ge(tiles_made, 1)
            e.dma_start(k.tile_d[0:1, :].rearrange("a t -> t a"), loi[0:NT, WGROUPS:WGROUPS + 1])\
             .then_inc(tiles_out, 16)
            e.dma_start(k.tile_d[1:2, :].rearrange("a t -> t a"), smaxi[:, :]).then_inc(tiles_out, 16)
            e.wait_ge(tiles_out, 32)
            e.dma_start(k.tlo[:, :], k.tile_d[0:1, :]).then_inc(rows_in, 16)
            e.dma_start(k.tspan[:, :], k.tile_d[1:2, :]).then_inc(rows_in, 16)
            e.wait_ge(rows_in, 48)

        @block.gpsimd
        def _(e):
            e.memset(identz[:, :], 0.0).then_inc(consts, 1)
            e.iota(k.iota[:, :], [[1, P]], base=0, channel_multiplier=0, allow_small_or_imprecise_dtypes=True)\
             .then_inc(consts, 1)
            e.iota(lob[:, 0:WGROUPS], [[WIN * WPG, WGROUPS]], base=0, channel_multiplier=WIN,
                   allow_small_or_imprecise_dtypes=True).then_inc(consts, 1)
            e.iota(hib[:, 0:WGROUPS], [[WIN * WPG, WGROUPS]], base=WIN - 1, channel_multiplier=WIN,
                   allow_small_or_imprecise_dtypes=True).then_inc(consts, 1)
            e.iota(lob[:, WGROUPS:], [[0, 1]], base=0, channel_multiplier=P,
                   allow_small_or_imprecise_dtypes=True).then_inc(consts, 1)
            e.iota(hib[:, WGROUPS:], [[0, 1]], base=P - 1, channel_multiplier=P,
                   allow_small_or_imprecise_dtypes=True).then_inc(consts, 1)
            e.memset(eps[:, :], BN_EPS).then_inc(consts, 1)
            e.wait_ge(consts, 7)
            e.affine_select(out=k.ident[:, :], in_=identz[:, :], compare_op=ALU.not_equal, fill=1.0, base=0,
                            pattern=[[-1, P]], channel_multiplier=1).then_inc(consts, 1)
            e.iota(desc, [[-1, CHUNKS]], base=CHUNKS, channel_multiplier=0,
                   allow_small_or_imprecise_dtypes=True).then_inc(consts, 1)
            e.iota(k.iota16[:, :], [[1, WC]], base=0, channel_multiplier=0,
                   allow_small_or_imprecise_dtypes=True).then_inc(consts, 1)
            e.iota(k.iota8[:, :], [[1, RELATIONS]], base=0, channel_multiplier=0,
                   allow_small_or_imprecise_dtypes=True).then_inc(consts, 1)
            e.iota(k.rank8[:, :], [[1, RELATIONS]], base=1, channel_multiplier=0,
                   allow_small_or_imprecise_dtypes=True).then_inc(consts, 1)
            e.memset(k.lneps[:, :], LN_EPS).then_inc(consts, 1)
            e.iota(k.wbase[:, :, :].rearrange("p t q -> p (t q)"), [[WIN, NW]], base=0, channel_multiplier=0,
                   allow_small_or_imprecise_dtypes=True).then_inc(consts, 1)
            e.iota(k.tbase[:, :], [[-P, NT]], base=0, channel_multiplier=0,
                   allow_small_or_imprecise_dtypes=True).then_inc(consts, 1)
            e.wait_ge(rec_out, 16)
            e.iota(asc, [[1, CHUNKS]], base=1, channel_multiplier=0,
                   allow_small_or_imprecise_dtypes=True).then_inc(consts, 1)

        @block.scalar
        def _(e):
            for t, ap in ((wemb[:, :], a["L0_gnn_W_emb"]),
                          (bemb[:, :], a["L0_gnn_b_emb"].rearrange("(p a) -> p a", a=1)),
                          (bases[:, :, :, :], a["L0_gnn_bases"].rearrange("l b d f -> d l b f")),
                          (coe[:, :], a["L0_gnn_w_coe"].rearrange("l r b -> (l r b)").partition_broadcast(P)),
                          (k.loop[:, :, :], a["L0_gnn_self_loop"].rearrange("l d f -> d l f")),
                          *((bn[i][:, :, :], a["L0_gnn_bn_" + n].rearrange("l f -> (l f)").partition_broadcast(P)
                             .rearrange("p (l f) -> p l f", l=LAYERS))
                            for i, n in enumerate(("gamma", "beta", "mean", "var")))):
                e.dma_start(t, ap).then_inc(weights_in, 16)
            e.wait_ge(weights_in, 9 * 16)
            e.wait_ge(consts, 7)
            e.activation(bn[3][:, :, :], bn[3][:, :, :], ACT.Sqrt, bias=eps[:, 0:1]).then_inc(var_made, 1)
            with e.Fori(0, NSEG) as tb:
                e.wait_ge(ht_ps, tb + 1)
                e.wait_ge(t_ps, tb * SEG)
                e.activation(ht[:, :], ph[:, 0:SW], ACT.Identity, bias=bemb[:, 0:1]).then_inc(ht_sb, 1)
                for i in range(SEG):
                    t = tb * SEG + i
                    slot, uses, before = (2, 1, 0) if i == SEG - 1 else (i % 2, SEG // 2, i // 2)
                    e.wait_ge(t_ps, t + 1)
                    e.wait_ge(t_out[slot], (tb * uses + before) * 16)
                    e.activation(tsb[:, slot, :], pt[:, bass.ds(t & 1, 1), :].rearrange("p a c -> p (a c)"), ACT.Copy)
                    e.activation(k.self_[:, bass.ds(t, 1), :], pse[:, bass.ds(t & 1, 1), 0:D], ACT.Copy)
                    e.drain().then_inc(t_bank, 1)
                    e.wait_ge(t_bank, t + 3)
                    e.dma_start(k.table_d[0][bass.ds(t * (P * RELATIONS), P * RELATIONS), :]
                                .rearrange("(p r) f -> p (r f)", r=RELATIONS), tsb[:, slot, :]).then_inc(t_out[slot], 16)
            for i in range(TSLOTS):
                e.wait_ge(t_out[i], NSEG * (SEG // 2 if i < 2 else 1) * 16)

        @block.tensor
        def _(e):
            e.wait_ge(x_in, 16)
            e.wait_ge(weights_in, 9 * 16)
            e.sem_inc(t_bank, 2)
            with e.Fori(0, NSEG) as tb:
                e.wait_ge(ht_sb, tb)
                for h in range(2):
                    m = e.matmul(ph[:, h * 512:h * 512 + (512, SW - 512)[h]], wemb[:, :],
                                 xt[:, bass.ds(tb * SW + h * 512, (512, SW - 512)[h])], start=True, stop=True)
                m.then_inc(ht_ps, 1)
                e.wait_ge(ht_sb, tb + 1)
                e.wait_ge(wr_made, 1)
                for i in range(SEG):
                    t = tb * SEG + i
                    e.wait_ge(t_bank, t + 1)
                    for h in range(2):
                        e.matmul(pt[:, bass.ds(t & 1, 1), h * 512:(h + 1) * 512], ht[:, i * P:(i + 1) * P],
                                 k.wr[:, 0, h * 512:(h + 1) * 512], start=True, stop=True)
                    e.matmul(pse[:, bass.ds(t & 1, 1), 0:D], ht[:, i * P:(i + 1) * P], k.loop[:, 0, :],
                             start=True, stop=True).then_inc(t_ps, 1)

        @block.vector
        def _(e):
            e.wait_ge(weights_in, 9 * 16)
            for b in range(BASES):
                for l in range(LAYERS):
                    for r in range(RELATIONS):
                        w = k.wr[:, l, r * D:(r + 1) * D]
                        c = coe[:, (l * RELATIONS + r) * BASES + b:(l * RELATIONS + r) * BASES + b + 1]
                        if b == 0:
                            e.tensor_scalar(w, bases[:, l, b, :], c, None, ALU.mult)
                        else:
                            e.scalar_tensor_tensor(w, bases[:, l, b, :], c, w, ALU.mult, ALU.add)
                e.drain()
            e.sem_inc(wr_made, 1)
            e.wait_ge(edges_in, 48)
            e.tensor_copy(dstf, dst)
            e.tensor_scalar(itmp, src, P - 1, None, ALU.bitwise_and)
            e.drain()
            for m, op in enumerate((ALU.min, ALU.max)):
                e.tensor_reduce(cm[:, m, :], dstf.rearrange("p (c i) -> p c i", i=CHUNK), AX.X, op)
            e.drain().then_inc(rec_made, 1)
            e.tensor_copy(rec[:, :, 0], dstf)
            e.tensor_copy(rec[:, :, 1], itmp)
            e.tensor_copy(rec[:, :, 3], typ)
            e.drain()
            e.tensor_scalar(itmp, src, 7, 3, ALU.logical_shift_right, ALU.logical_shift_left)
            e.tensor_scalar(dst, src, 3, None, ALU.logical_shift_left)
            e.drain()
            e.tensor_copy(rec[:, :, 2], itmp)
            e.tensor_tensor(rec[:, :, 4].bitcast(I32), dst, typ, ALU.bitwise_or)
            e.drain().then_inc(rec_made, 1)
            e.wait_ge(var_made, 1)
            e.reciprocal(bn[3][:, :, :], bn[3][:, :, :])
            e.drain()
            e.tensor_tensor(k.bns[:, :, :], bn[0][:, :, :], bn[3][:, :, :], ALU.mult)
            e.drain()
            e.tensor_tensor(bn[2][:, :, :], bn[2][:, :, :], k.bns[:, :, :], ALU.mult)
            e.drain()
            e.tensor_tensor(k.bnb[:, :, :], bn[1][:, :, :], bn[2][:, :, :], ALU.subtract)
            e.wait_ge(bounds_in, 16)
            e.wait_ge(rec_out, 16)
            e.wait_ge(consts, CONSTS)
            for g in range(WGROUPS + 1):
                e.scalar_tensor_tensor(scr[:, 0, :], bounds[:, 1, :], lob[:, g:g + 1], desc, ALU.is_ge, ALU.mult)
                e.scalar_tensor_tensor(scr[:, 1, :], bounds[:, 0, :], hib[:, g:g + 1], asc, ALU.is_le, ALU.mult)
                e.drain()
                e.reduce_max(m1[:, g:g + 1], scr[:, 0, :], AX.X)
                e.reduce_max(m2[:, g:g + 1], scr[:, 1, :], AX.X)
                e.drain()
            e.tensor_scalar(m1[:, :], m1[:, :], -1.0, float(CHUNKS), ALU.mult, ALU.add)
            e.drain()
            e.tensor_scalar(m1[:, :], m1[:, :], float(REAL_CHUNKS), None, ALU.min)
            e.drain()
            e.tensor_copy(loi[:, :], m1[:, :])
            e.tensor_tensor(wsp[:, :], m2[:, :], m1[:, :], ALU.subtract)
            e.drain().then_inc(spans_made, 1)
            e.wait_ge(spans_in, 16)
            e.reduce_max(smax[:, :], wt[:, :], AX.X)
            e.tensor_scalar(wsp[0:NT, WGROUPS:], wsp[0:NT, WGROUPS:], float(WIN_STEP), None, ALU.mult)
            e.drain()
            e.tensor_scalar(smax[:, :], smax[:, :], float(TILE_STEP), 1.0, ALU.mult, ALU.max)
            e.drain()
            e.tensor_tensor(smaxf[:, :], smax[:, :], wsp[0:NT, WGROUPS:], ALU.max)
            e.drain()
            e.tensor_copy(smaxi[:, :], smaxf[:, :])
            e.drain().then_inc(tiles_made, 1)
            e.tensor_copy(k.ident16[:, :], k.ident[:, :])
            e.wait_ge(rows_in, 48)
            e.tensor_copy(spanf[:, :], k.tspan[:, :])
            e.drain()
            e.reduce_max(mostf[:, :], spanf[:, :], AX.X)
            e.drain()
            e.tensor_copy(k.most[:, :], mostf[:, :])


WINDOWS = [2, 2, 2, 2, 2, 3, 3]


def counter(e, name):
    r = e.alloc_register(name)
    e.reg_mov(r, 0)
    return r


def phase_layer(nc, k, l):
    with ExitStack() as ctx:
        sb = lambda name, shape, dt=F32: ctx.enter_context(nc.sbuf_tensor(f"{name}_{l}", shape, dt))
        pb = lambda name, shape, dt=F32: ctx.enter_context(nc.psum_tensor(f"{name}_{l}", shape, dt))
        sem = lambda name: ctx.enter_context(nc.semaphore(f"l{l}_{name}"))
        first = l == 0
        gw = GW if first else D
        recs = sb("recs", [P, SLOTS, REC])
        rows = sb("rows", [P, SLOTS, gw])
        hot = sb("hot", [P, SLOTS, P])
        agg = sb("agg", [P, gw])
        h = sb("h", [P, D])
        acc = pb("acc", [P, 512])
        rec_in = [sem(f"rec_in{g}") for g in range(GROUPS)]
        gathered = [sem(f"gathered{g}") for g in range(GROUPS)]
        turn = sem("turn")
        ring, hot_made, acc_free = sem("ring"), sem("hot_made"), sem("acc_free")
        if first:
            wrec = sb("wrec", [P, WPT * WSLOTS, REC])
            key = sb("key", [P, WPT * WSLOTS])
            dloc = sb("dloc", [P, WPT * WSLOTS])
            inw = sb("inw", [P, WPT * WSLOTS])
            wlo = sb("wlo16", [P, WPT * WSLOTS])
            whot = sb("whot", [P, 4, WSLOTS, P], F16)
            wkey = sb("wkey", [P, 4, WSLOTS, WC], F16)
            both_rows = lambda w: cells(k.pair.rearrange("p a t f -> p (a t f)"), w).rearrange("p (a c) -> p a c", a=2)
            small = sb("small", [P, 4, RELATIONS])
            best = sb("best", [P, 1])
            ht = sb("ht", [P, P])
            tsb = sb("tsb", [P, TW])
            wps = pb("wps", [P, 4, 512])
            pm = pb("pm", [P, 512])
            pt = pb("pt", [P, 1024])
            attr_in = [sem(f"attr_in{g}") for g in range(GROUPS)]
            wrec_in, keys_made, whot_made = sem("wrec_in"), sem("keys_made"), sem("whot_made")
            counted, moved, stored, summed = sem("counted"), sem("moved"), sem("stored"), sem("summed")
            h_made, ht_ps, ht_sb = sem("h_made"), sem("ht_ps"), sem("ht_sb")
            t_ps, t_sb, t_out = sem("t_ps"), sem("t_sb"), sem("t_out")
        else:
            room = sb("csr", [P, NPAD])
            segments = lambda ap, w: cells(ap, w).rearrange("p (g c) -> p g c", g=NSEG)
            csr = {w: segments(room[:, :], w) for w in (True, False)}
            cdr = {w: segments(k.spare.rearrange("p t f -> p (t f)"), w) for w in (True, False)}
            pen = sb("pen", [P, NSEG, SW], BF16)
            banks = pb("tps", [P, 3, 1024])
            tps = {w: [cells(banks[:, i, 0:SW], w) for i in range(3)] for w in (True, False)}
            cs_in = [sem(f"cs_in{g}") for g in range(GROUPS)]
            stored = [sem(f"stored{g}") for g in range(GROUPS)]
            turned, moved, pen_made, x_in = sem("turned"), sem("moved"), sem("pen_made"), sem("x_in")
            attr_out = sem("attr_out")
        block = ctx.enter_context(nc.Block())

        def rounds(e, body, before=None, after=None, wide=False):
            done = counter(e, f"rounds_{l}_{wide}")
            with e.Fori(0, NT) as t:
                if before:
                    before(t)
                span = e.value_load(k.tspan[0:1, bass.ds(t, 1)], min_val=1, max_val=CHUNKS * TILE_STEP)
                with e.Fori(0, span, WIN_STEP * TILE_STEP) as r:
                    body(t, r, e.snap(done, min_val=0, max_val=1 << 20))
                    e.reg_add(done, done, 1)
                if after:
                    after(t)
            return e.snap(done, min_val=0, max_val=1 << 20)

        @block.sync
        def _(e):
            if not first:
                e.dma_start(k.x[:, :, :], k.ins["x"].rearrange("(t p) f -> p t f", p=P)).then_inc(x_in, 16)
                e.dma_start(k.attr_d, k.attr[:, :, :].rearrange("p t f -> p (t f)")).then_inc(attr_out, 16)
            at = e.alloc_register(f"tile_chunk_{l}")
            wat = e.alloc_register(f"window_offset_{l}")
            wch = e.alloc_register(f"window_chunk_{l}")

            def before(t):
                e.reg_mov(at, e.value_load(k.tlo[0:1, bass.ds(t, 1)], min_val=0, max_val=REAL_CHUNKS))
                e.reg_mov(wat, 0)

            def body(t, r, b, wide):
                if first:
                    for q in range(WPT):
                        lo = e.value_load(k.wlo[0:1, bass.ds(t * WPT + q, 1)], min_val=0, max_val=REAL_CHUNKS)
                        e.reg_mov(wch, lo)
                        e.reg_add(wch, wch, wat)
                        e.reg_alu(wch, wch, CHUNKS - WIN_STEP, ALU.min)
                        c = e.snap(wch, min_val=0, max_val=CHUNKS - WIN_STEP)
                        e.wait_ge(keys_made, b)
                        e.dma_start(wrec[:, q * WSLOTS:(q + 1) * WSLOTS, :].rearrange("p a b -> p (a b)"),
                                    k.rec_d[bass.ds(c * (CHUNK * REC), P * WSLOTS * REC)]
                                    .rearrange("(p c) -> p c", p=P)).then_inc(wrec_in, 16)
                    e.reg_add(wat, wat, WIN_STEP)
                c = e.snap(at, min_val=0, max_val=REAL_CHUNKS)
                for g in range(GROUPS):
                    e.wait_ge(ring, b * GROUPS + (g + 1))
                    s = slice(g * PER, (g + 1) * PER)
                    e.dma_start(recs[:, s, :].rearrange("p a b -> p (a b)"),
                                k.rec_d[bass.ds(c * (CHUNK * REC), P * SLOTS * REC)]
                                .rearrange("(p c) -> p c", p=P)[:, g * PER * REC:(g + 1) * PER * REC])\
                     .then_inc(rec_in[g], 16)
                    if first:
                        e.dma_start(rows[:, s, D:2 * D],
                                    k.ins["edge_attr_128"][bass.ds(c * CHUNK, P * SLOTS), :]
                                    .rearrange("(p j) f -> p j f", p=P)[:, s, :]).then_inc(attr_in[g], 16)
                    else:
                        e.wait_ge(turned, b * GROUPS + (g + 1))
                        e.dma_start(csr[wide][:, g, :], k.cs_d[wide][bass.ds(t, 1), :, g * SW:(g + 1) * SW]
                                    .rearrange("a p c -> (a p) c")).then_inc(cs_in[g], 16)
                e.reg_add(at, at, TILE_STEP)
                e.reg_alu(at, at, REAL_CHUNKS, ALU.min)

            def program(wide):
                rounds(e, lambda t, r, b: body(t, r, b, wide), before, wide=wide)

            if first:
                program(False)
            else:
                either(e, k, program)
                e.wait_ge(attr_out, 16)

        @block.gpsimd
        def _(e):
            def body(t, r, b):
                for g in range(GROUPS):
                    e.wait_ge(rec_in[g], (b + 1) * 16)
                    e.wait_ge(ring, b * GROUPS + (g + 1))
                    e.sem_inc(turn, 1)
                    for j in range(g * PER, (g + 1) * PER):
                        e.indirect_dma_start(
                            out=rows[:, j, 0:D], out_offset=None, in_=k.table_d[l],
                            in_offset=bass.IndirectOffsetOnAxis(ap=recs[:, j, 4:5].bitcast(I32), axis=0),
                        ).then_inc(gathered[g], 16)

            rounds(e, body)

        @block.tensor
        def _(e):
            e.sem_inc(ring, GROUPS)
            if first:
                e.sem_inc(counted, 4)
            else:
                e.sem_inc(turned, GROUPS)

            def body(t, r, b, wide):
                q = 0
                for g in range(GROUPS):
                    if not first:
                        e.wait_ge(cs_in[g], (b + 1) * 16)
                        e.wait_ge(moved, b * GROUPS + max(0, g - 2))
                        for i in range(SEG):
                            m = e.transpose(tps[wide][g % 3][:, i * P:(i + 1) * P], csr[wide][:, g, i * P:(i + 1) * P],
                                            (k.ident if wide else k.ident16)[:, :])
                        m.then_inc(turned, 1)
                    e.wait_ge(gathered[g], (b + 1) * (16 * PER))
                    e.wait_ge(hot_made, b * GROUPS + (g + 1))
                    if first:
                        e.wait_ge(attr_in[g], (b + 1) * 16)
                    if g == 0:
                        e.wait_ge(acc_free, b)
                    for j in range(g * PER, (g + 1) * PER):
                        m = e.matmul(acc[:, 0:gw], hot[:, j, :], rows[:, j, :], start=j == 0, stop=j == SLOTS - 1)
                    m.then_inc(ring, 1)
                    if not first:
                        continue
                    for _ in range(WINDOWS[g]):
                        e.wait_ge(whot_made, b * WPT + (q + 1))
                        e.wait_ge(moved, b * WPT + (q + 1))
                        for j in range(WSLOTS):
                            m = e.matmul(wps[:, q % 4, 0:WC], whot[:, q % 4, j, :], wkey[:, q % 4, j, :],
                                         start=j == 0, stop=j == WSLOTS - 1)
                        m.then_inc(counted, 1)
                        q += 1

            def after(t):
                e.wait_ge(h_made, t + 1)
                e.wait_ge(t_sb, t)
                e.transpose(pm[:, 0:P], h[:, :], k.ident[:, :]).then_inc(ht_ps, 1)
                e.wait_ge(ht_sb, t + 1)
                for i in range(2):
                    e.matmul(pt[:, i * 512:(i + 1) * 512], ht[:, :], k.wr[:, 1, i * 512:(i + 1) * 512],
                             start=True, stop=True)
                e.matmul(pm[:, P:2 * P], ht[:, :], k.loop[:, 1, :], start=True, stop=True).then_inc(t_ps, 1)

            def program(wide):
                rounds(e, lambda t, r, b: body(t, r, b, wide), after=after if first else None, wide=wide)

            if first:
                program(False)
            else:
                either(e, k, program)

        @block.scalar
        def _(e):
            if first:
                e.sem_inc(moved, 4)

            def body(t, r, b, wide):
                if not first:
                    for g in range(GROUPS):
                        e.wait_ge(turned, b * GROUPS + (g + 1 + GROUPS))
                        e.wait_ge(stored[g], b * 32)
                        e.wait_ge(pen_made, b * GROUPS + (g + 1))
                        e.activation(cdr[wide][:, g, :], tps[wide][g % 3], ACT.Copy).then_inc(moved, 1)
                        e.wait_ge(moved, b * GROUPS + (g + 1))
                        e.dma_start(k.cd_d[wide][bass.ds(t, 1), :, g * SW:(g + 1) * SW].rearrange("a p c -> (a p) c"),
                                    cdr[wide][:, g, :]).then_inc(stored[g], 16)
                        e.wait_ge(pen_made, b * GROUPS + (g + 1 + GROUPS))
                        e.dma_start(k.pen_d[bass.ds(t, 1), :, g * SW:(g + 1) * SW].rearrange("a p c -> (a p) c"),
                                    pen[:, g, :]).then_inc(stored[g], 16)
                    return
                mine = both_rows(wide)[:, bass.ds(b & 1, 1), :].rearrange("p a c -> p (a c)")
                for q in range(WPT):
                    e.wait_ge(counted, b * WPT + (q + 1 + 4))
                    e.activation(mine.rearrange("p (c d) -> p c d", d=P)[:, :, q * WIN:(q + 1) * WIN],
                                 wps[:, q % 4, 0:WC].rearrange("p (c w) -> p c w", w=WIN), ACT.Copy).then_inc(moved, 1)
                e.wait_ge(moved, b * WPT + (WPT + 4))
                e.wait_ge(summed, b + 1)
                e.wait_ge(stored, b * 16)
                e.dma_start(k.cs_d[wide][bass.ds(t, 1), :, :].rearrange("a p c -> (a p) c"), mine).then_inc(stored, 16)

            def after(t):
                e.wait_ge(ht_ps, t + 1)
                e.activation(ht[:, :], pm[:, 0:P], ACT.Copy).then_inc(ht_sb, 1)
                e.wait_ge(t_ps, t + 1)
                e.wait_ge(t_out, t * 16)
                e.activation(tsb[:, :], pt[:, :], ACT.Copy)
                e.activation(k.self_[:, bass.ds(t, 1), :], pm[:, P:2 * P], ACT.Copy).then_inc(t_sb, 1)
                e.wait_ge(t_sb, t + 1)
                e.dma_start(k.table_d[1][bass.ts(t, P * RELATIONS), :].rearrange("(p r) f -> p (r f)", r=RELATIONS),
                            tsb[:, :]).then_inc(t_out, 16)

            def program(wide):
                total = rounds(e, lambda t, r, b: body(t, r, b, wide), after=after if first else None, wide=wide)
                if first:
                    e.wait_ge(t_out, NT * 16)
                    e.wait_ge(stored, total * 16)
                else:
                    for g in range(GROUPS):
                        e.wait_ge(stored[g], total * 32)
                    roots(e, k, 1)
                e.sem_inc(turn, 1)

            either(e, k, program)

        @block.vector
        def _(e):
            if not first:
                e.sem_inc(pen_made, GROUPS)
                e.wait_ge(x_in, 16)

            def before(t):
                e.memset(agg[:, :], 0.0)

            def keys(t, b):
                e.wait_ge(wrec_in, (b + 1) * (16 * WPT))
                dl = dloc[:, :].rearrange("p (q j) -> p q j", j=WSLOTS)
                e.tensor_tensor(dl, wrec[:, :, 0].rearrange("p (q j) -> p q j", j=WSLOTS),
                                spread(k.wbase[:, bass.ds(t, 1), :].rearrange("p a q -> p (a q)"), WSLOTS), ALU.subtract)
                e.tensor_copy(wlo[:, :], wrec[:, :, 1])
                e.drain()
                e.tensor_scalar(inw[:, :], dloc[:, :], 0.0, None, ALU.is_ge)
                e.scalar_tensor_tensor(key[:, :], dloc[:, :], 1.0, wrec[:, :, 2], ALU.add, ALU.add)
                e.drain()
                e.scalar_tensor_tensor(inw[:, :], dloc[:, :], float(WIN), inw[:, :], ALU.is_lt, ALU.mult)
                e.drain()
                e.tensor_tensor(key[:, :], key[:, :], inw[:, :], ALU.mult)
                e.drain()
                e.tensor_scalar(key[:, :], key[:, :], -1.0, None, ALU.add)
                e.drain().then_inc(keys_made, 1)

            def body(t, r, b, wide):
                if first:
                    keys(t, b)
                q = 0
                base = k.tbase[:, bass.ds(t, 1)]
                for g in range(GROUPS):
                    e.wait_ge(rec_in[g], (b + 1) * 16)
                    e.wait_ge(ring, b * GROUPS + (g + 1))
                    for j in range(g * PER, (g + 1) * PER):
                        m = e.tensor_scalar(hot[:, j, :], k.iota[:, :], recs[:, j, 0:1], base,
                                            ALU.subtract, ALU.is_equal)
                    if first:
                        s = slice(g * PER, (g + 1) * PER)
                        m = e.tensor_tensor(rows[:, s, 2 * D:], repeat(k.iota8[:, :], PER),
                                            spread(recs[:, s, 3], RELATIONS), ALU.is_equal)
                    m.then_inc(hot_made, 1)
                    if not first:
                        e.wait_ge(moved, b * GROUPS + (g + 1))
                        e.tensor_scalar(pen[:, g, :], cdr[wide][:, g, :], 0.0, FAR, ALU.is_equal, ALU.mult)\
                         .then_inc(pen_made, 1)
                        continue
                    for _ in range(WINDOWS[g]):
                        e.wait_ge(counted, b * WPT + (q + 1))
                        for j in range(WSLOTS):
                            i = q * WSLOTS + j
                            e.tensor_scalar(whot[:, q % 4, j, :], k.iota16[:, 0:P], wlo[:, i:i + 1], None, ALU.is_equal)
                            m = e.tensor_scalar(wkey[:, q % 4, j, :], k.iota16[:, :], key[:, i:i + 1], None, ALU.is_equal)
                        m.then_inc(whot_made, 1)
                        q += 1
                e.drain()
                e.wait_ge(ring, b * GROUPS + 2 * GROUPS)
                e.tensor_tensor(agg[:, :], agg[:, :], acc[:, 0:gw], ALU.add).then_inc(acc_free, 1)
                if first:
                    with e.If(r > 0):
                        e.wait_ge(moved, b * WPT + (WPT + 4))
                        mine, other = (both_rows(wide)[:, bass.ds((b + i) & 1, 1), :].rearrange("p a c -> p (a c)")
                                       for i in range(2))
                        e.tensor_tensor(mine, mine, other, ALU.add)
                    e.drain().then_inc(summed, 1)

            def after(t):
                e.drain()
                norm = k.norm[:, bass.ds(t, 1)]
                if first:
                    count = agg[:, 2 * D:]
                    e.tensor_scalar(small[:, 0, :], count, 1.0, None, ALU.max)
                    e.scalar_tensor_tensor(small[:, 1, :], count, 0.0, k.rank8[:, :], ALU.is_gt, ALU.mult)
                    e.tensor_copy(k.attr[:, bass.ds(t, 1), :].rearrange("p a f -> p (a f)"), agg[:, D:2 * D])
                    e.drain()
                    e.reciprocal(small[:, 2, :], small[:, 0, :])
                    e.reduce_max(best[:, :], small[:, 1, :], AX.X)
                    e.drain()
                    e.scalar_tensor_tensor(small[:, 3, :], count, 0.0, small[:, 2, :], ALU.is_gt, ALU.mult)
                    e.drain()
                    e.scalar_tensor_tensor(small[:, 2, :], small[:, 1, :], best[:, 0:1], small[:, 3, :],
                                           ALU.is_equal, ALU.mult)
                    e.drain()
                    e.reduce_sum(norm, small[:, 2, :], AX.X)
                    e.drain()
                    e.wait_ge(ht_ps, t)
                e.scalar_tensor_tensor(h[:, :], agg[:, 0:D], norm, k.self_[:, bass.ds(t, 1), :].rearrange("p a f -> p (a f)"),
                                       ALU.mult, ALU.add)
                e.drain()
                e.tensor_tensor(h[:, :], h[:, :], k.bns[:, l, :], ALU.mult)
                e.drain()
                e.tensor_tensor(h[:, :], h[:, :], k.bnb[:, l, :], ALU.add)
                e.drain()
                if first:
                    e.tensor_scalar(h[:, :], h[:, :], 0.0, None, ALU.max).then_inc(h_made, 1)
                    return
                x = k.x[:, bass.ds(t, 1), :].rearrange("p a f -> p (a f)")
                e.scalar_tensor_tensor(x, h[:, :], 0.0, x, ALU.max, ALU.add)
                e.drain()
                tile_stats(e, k, x, t)

            either(e, k, lambda wide: rounds(e, lambda t, r, b: body(t, r, b, wide), before, after, wide))
            if not first:
                normalize(e, k, 1)


def tile_stats(e, k, x, t):
    e.bn_stats(k.stat[:, :], x)
    e.drain()
    e.bn_aggr(k.mv1[:, :], k.stat[:, :])
    e.drain()
    e.tensor_copy(k.mv[:, bass.ds(t, 1), :].rearrange("p a c -> p (a c)"), k.mv1[:, :])


def roots(e, k, nth):
    e.wait_ge(k.vars_made, nth)
    e.activation(k.rstd[:, :], k.mv[:, :, 1], ACT.Sqrt, bias=k.lneps[:, 0:1]).then_inc(k.roots_made, 1)


def normalize(e, k, nth, made=None, rows=None):
    e.drain().then_inc(k.vars_made, 1)
    e.wait_ge(k.roots_made, nth)
    e.reciprocal(k.rstd[:, :], k.rstd[:, :])
    e.drain()
    x = (k.x if rows is None else rows)[:, :, :]
    e.tensor_tensor(x, x, spread(k.mv[:, :, 0], D), ALU.subtract)
    e.drain()
    m = e.tensor_tensor(x, x, spread(k.rstd[:, :], D), ALU.mult)
    if made:
        m.then_inc(made, 1)


def phase_sum_to_source(nc, k):
    with ExitStack() as ctx:
        sb = lambda name, shape, dt=F32: ctx.enter_context(nc.sbuf_tensor("s_" + name, shape, dt))
        sem = lambda name: ctx.enter_context(nc.semaphore("s_" + name))
        room = sb("ring", [P, SEG, HALF])
        ring = {w: [cells(room[:, i, :], w) for i in range(SEG)] for w in (True, False)}
        xl = sb("xl", [P, SEG, D])
        parts = sb("parts", [P, NT, 2 * D], F16)
        rest = sb("rest", [P, SEG, D])
        acc = ctx.enter_context(nc.psum_tensor("s_acc", [P, 8, 512], F32))
        total = k.self_[:, :, :].rearrange("p t f -> p (t f)")
        rows_in = [sem(f"rows_in{i}") for i in range(SEG)]
        parts_made = sem("parts_made")
        xl_made, used, emptied, turned, taken = sem("xl_made"), sem("used"), sem("emptied"), sem("turned"), sem("taken")
        block = ctx.enter_context(nc.Block())

        @block.sync
        def _(e):
            def program(wide):
                for h in range(2):
                    with e.Fori(0, NSEG) as tb:
                        for i in range(SEG):
                            e.wait_ge(used, tb * SEG + (h * NT + i + 1))
                            e.dma_start(ring[wide][i], k.cd_d[wide][bass.ds(tb * SEG + i, 1), :, h * HALF:(h + 1) * HALF]
                                        .rearrange("a p c -> (a p) c")).then_inc(rows_in[i], 16)

            either(e, k, program)

        @block.gpsimd
        def _(e):
            def program(wide):
                if not wide:
                    e.sem_inc(xl_made, 1)
                    return
                for h in range(2):
                    with e.Fori(0, NSEG) as tb:
                        for i in range(SEG):
                            e.wait_ge(used, tb * SEG + (h * NT + i + 1))
                            e.tensor_copy(xl[:, i, :], k.x[:, bass.ds(tb * SEG + i, 1), :].rearrange("p a f -> p (a f)"))\
                             .then_inc(xl_made, 1)

            either(e, k, program)

        @block.tensor
        def _(e):
            e.sem_inc(used, SEG)

            def batch(wide, h, tb, start, stop):
                for i in range(SEG):
                    e.wait_ge(rows_in[i], (tb + (h * NSEG + 1)) * 16)
                    if wide:
                        e.wait_ge(xl_made, tb * SEG + (h * NT + i + 1))
                        weights = [xl[:, i, :]]
                    else:
                        if not h:
                            e.wait_ge(parts_made, tb + 1)
                        weights = [parts[:, bass.ds(tb * SEG + i, 1), q * D:(q + 1) * D].rearrange("p a f -> p (a f)")
                                   for q in range(2)]
                    for q, w in enumerate(weights):
                        for s in range(NSEG):
                            m = e.matmul(acc[:, s, 0:HSEG], w, ring[wide][i][:, s * HSEG:(s + 1) * HSEG],
                                         start=start and i == 0 and q == 0,
                                         stop=stop and i == SEG - 1 and q == len(weights) - 1)
                    m.then_inc(used, 1)

            def program(wide):
                for h in range(2):
                    if h:
                        e.wait_ge(emptied, NSEG)
                    batch(wide, h, 0, True, False)
                    with e.Fori(1, NSEG - 1) as tb:
                        batch(wide, h, tb, False, False)
                    batch(wide, h, NSEG - 1, False, True)

            either(e, k, program)
            e.wait_ge(emptied, 2 * NSEG)
            for t in range(NT):
                if t >= 2 * SEG and t % SEG == 0:
                    e.wait_ge(taken, t // SEG - 1)
                b = t // SEG % 2
                m = e.transpose(acc[:, 2 * b:2 * b + 2, :].rearrange("p a c -> p (a c)")[:, t % SEG * P:(t % SEG + 1) * P],
                                total[:, t * P:(t + 1) * P], k.ident[:, :])
                if t % SEG == SEG - 1:
                    m.then_inc(turned, 1)

        @block.scalar
        def _(e):
            def program(wide):
                for h in range(2):
                    e.wait_ge(used, SEG + (h + 1) * NT)
                    for s in range(NSEG // 2, NSEG):
                        e.activation(total[:, h * HALF + s * HSEG:h * HALF + (s + 1) * HSEG], acc[:, s, 0:HSEG], ACT.Copy,
                                     scale=1.0 if wide else 1 / SCALE).then_inc(emptied, 1)

            either(e, k, program)
            roots(e, k, 2)

        @block.vector
        def _(e):
            with e.Fori(0, NSEG) as tb:
                split_rows(e, k.x, parts, rest[:, :, :], tb, parts_made)

            def program(wide):
                for h in range(2):
                    e.wait_ge(used, SEG + (h + 1) * NT)
                    for s in range(NSEG // 2):
                        e.tensor_scalar(total[:, h * HALF + s * HSEG:h * HALF + (s + 1) * HSEG], acc[:, s, 0:HSEG],
                                        1.0 if wide else 1 / SCALE, None, ALU.mult).then_inc(emptied, 1)

            either(e, k, program)
            with e.Fori(0, NSEG) as tb:
                e.wait_ge(turned, tb + 1)
                x = k.x[:, bass.ts(tb, SEG), :].rearrange("p a f -> p (a f)")
                e.scalar_tensor_tensor(x, x, 2.0, acc[:, bass.ds((tb & 1) * 2, 2), :].rearrange("p a c -> p (a c)")[:, 0:SW],
                                       ALU.mult, ALU.add).then_inc(taken, 1)
                e.drain()
                batch_stats(e, k, k.x, tb)
            normalize(e, k, 2)


def batch_stats(e, k, x, tb):
    for i in range(SEG):
        e.bn_stats(k.stat7[:, i, :], x[:, bass.ds(tb * SEG + i, 1), :].rearrange("p a f -> p (a f)"))
    e.drain()
    for i in range(SEG):
        e.bn_aggr(k.mv7[:, i, :], k.stat7[:, i, :])
    e.drain()
    e.tensor_copy(k.mv[:, bass.ds(tb * SEG, SEG), :], k.mv7[:, :, :])
    e.drain()


def phase_attention(nc, k):
    with ExitStack() as ctx:
        sb = lambda name, shape, dt=F32: ctx.enter_context(nc.sbuf_tensor("a_" + name, shape, dt))
        pb = lambda name, shape, dt=F32: ctx.enter_context(nc.psum_tensor("a_" + name, shape, dt))
        sem = lambda name: ctx.enter_context(nc.semaphore("a_" + name))
        wide = 2 * D + 2
        wmsg = sb("wmsg", [P, D])
        attn = sb("attn", [P, 2])
        wcat = sb("wcat", [P, wide])
        wfrom = sb("wfrom", [P, P])
        coef = sb("coef", [P, 1])
        sig = sb("sig", [P, 1])
        score = sb("score", [P, 2, NT])
        leaky_from = sb("leaky_from", [P, 3, NT])
        frow = k.self_[:, :, :].rearrange("p t f -> p (t f)")
        pen = sb("pen", [P, 2, NPAD], BF16)
        best = sb("best", [P, SEG])
        t7 = sb("t7", [P, 4, SEG])
        diag = sb("diag", [P, 2, SEG, P])
        leaky_to = diag[:, 1, :, :].rearrange("p i c -> p (i c)")
        ones = sb("ones", [P, P])
        room = sb("counts", [P, 2, SEG * SW])
        counts = {w: [cells(room[:, i, :], w).rearrange("p (t c) -> p t c", t=SEG) for i in range(2)] for w in (True, False)}
        powers = sb("powers", [P, 4, SW])
        xs, xt = powers[:, 0, :], powers[:, 1, :]
        weights = sb("weights", [P, SEG, SW])
        den = sb("den", [P, SEG])
        fresh = sb("fresh", [P, SEG, D])
        weights_in, wcat_ps, wcat_made, consts = sem("weights_in"), sem("wcat_ps"), sem("wcat_made"), sem("consts")
        coef_exp, sig_made = sem("coef_exp"), sem("sig_made")
        xs_made, xt_ps, xt_sb = sem("xs_made"), sem("xt_ps"), sem("xt_sb")
        msg_ps, msg_act, msg_dve, frow_ps, frow_sb = sem("msg_ps"), sem("msg_act"), sem("msg_dve"), sem("frow_ps"), sem("frow_sb")
        pen_in = [sem(f"pen_in{i}") for i in range(2)]
        counts_in = [sem(f"counts_in{i}") for i in range(2)]
        pen_used, diag_made, uv_made = sem("pen_used"), sem("diag_made"), sem("uv_made")
        powered, summed, closed = sem("powered"), sem("summed"), sem("closed")
        leaky_moved, exponents, weighed, pool_weighed = sem("leaky_moved"), sem("exponents"), sem("weighed"), sem("pool_weighed")

        turn, dve_turn, pool_turn = sem("turn"), sem("dve_turn"), sem("pool_turn")

        def wait_weighed(e, chunk, j):
            if j in ON_POOL:
                e.wait_ge(pool_weighed, chunk * len(ON_POOL) + ON_POOL.index(j) + 1)
            else:
                e.wait_ge(weighed, chunk * (SEG - len(ON_POOL)) + (j - sum(i < j for i in ON_POOL) + 1))

        psum = pb("psum", [P, 8, 512])
        bank2 = lambda i: psum[:, i:i + 2, :].rearrange("p a c -> p (a c)")
        block = ctx.enter_context(nc.Block())

        @block.sync
        def _(e):
            for t, ap in ((wmsg[:, :], k.ins["w_msg"]),
                          (attn[:, :], k.ins["attn_w"].rearrange("(c p) -> p c", c=2)),
                          (wcat[:, 0:D], k.ins["w_msg_transposed"]),
                          (wcat[:, D + 2:], k.ins["w_res_transposed"]),
                          (coef[:, :], k.ins["coef"].partition_broadcast(P))):
                e.dma_start(t, ap, allow_slow_non_contiguous=True).then_inc(weights_in, 16)
            def penalties(tg, i):
                e.wait_ge(pen_used, tg * SEG + max(0, i - 1))
                e.dma_start(pen[:, i % 2, :], k.pen_d[bass.ds(tg * SEG + i, 1), :, :].rearrange("a p c -> (a p) c"))\
                 .then_inc(pen_in[i % 2], 16)

            def group(wide, tg, last):
                for hb in range(NSEG):
                    e.wait_ge(weighed, tg * (NSEG * (SEG - len(ON_POOL))) + max(0, hb - 1) * (SEG - len(ON_POOL)))
                    e.sem_inc(turn, 1)
                    e.wait_ge(pool_weighed, tg * (NSEG * len(ON_POOL)) + max(0, hb - 1) * len(ON_POOL))
                    e.sem_inc(turn, 1)
                    e.dma_start(counts[wide][hb % 2], k.cs_d[wide][bass.ds(tg * SEG, SEG), :, hb * SW:(hb + 1) * SW]
                                .rearrange("t p c -> p t c")).then_inc(counts_in[hb % 2], 16)
                    if not last:
                        penalties(tg + 1, hb)

            def program(wide):
                with e.Fori(0, NSEG - 1) as tg:
                    group(wide, tg, False)
                group(wide, NSEG - 1, True)

            for i in range(SEG):
                penalties(0, i)
            either(e, k, program)

        @block.gpsimd
        def _(e):
            e.memset(ones[:, :], 1.0).then_inc(consts, 1)
            e.memset(k.msg[:, :, D:D + 1], 1.0).then_inc(consts, 1)
            with e.Fori(0, NSEG) as tb:
                e.wait_ge(xt_ps, tb)
                e.tensor_copy(xs, k.x[:, bass.ts(tb, SEG), :].rearrange("p a f -> p (a f)")).then_inc(xs_made, 1)

            def program(wide):
                with e.Fori(0, NSEG) as tg:
                    for hb in range(NSEG):
                        for j in ON_POOL:
                            n = tg * NT + (hb * SEG + j)
                            e.wait_ge(counts_in[hb % 2], (tg * (4 - hb % 2) + (hb // 2 + 1)) * 16)
                            e.wait_ge(powered, n + 1)
                            e.wait_ge(summed, tg * NT + max(0, hb * SEG + j - SEG + 1))
                            e.sem_inc(pool_turn, 1)
                            e.tensor_tensor(weights[:, j, :].rearrange("p (i c) -> p i c", c=P),
                                            powers[:, bass.ds(n & 3, 1), :].rearrange("p a (i c) -> p (a i) c", c=P),
                                            counts[wide][hb % 2][:, :, j * P:(j + 1) * P], ALU.mult)\
                             .then_inc(pool_weighed, 1)

            either(e, k, program)

        @block.tensor
        def _(e):
            e.wait_ge(weights_in, 5 * 16)
            e.matmul(psum[:, 0, 0:2], wmsg[:, :], attn[:, :], start=True, stop=True).then_inc(wcat_ps, 1)
            e.wait_ge(wcat_made, 1)
            with e.Fori(0, NSEG) as tb:
                e.wait_ge(xs_made, tb + 1)
                e.wait_ge(xt_sb, tb)
                for i in range(SEG):
                    m = e.transpose(bank2(0)[:, i * P:(i + 1) * P], xs[:, i * P:(i + 1) * P], k.ident[:, :])
                m.then_inc(xt_ps, 1)
                e.wait_ge(xt_sb, tb + 1)
                e.wait_ge(frow_sb, tb)
                for s in range(2):
                    m = e.matmul(psum[:, 2 + s, 0:SW // 2], wfrom[:, :], xt[:, s * SW // 2:(s + 1) * SW // 2],
                                 start=True, stop=True)
                m.then_inc(frow_ps, 1)
                for i in range(SEG):
                    e.wait_ge(msg_dve, tb * SEG + max(0, i - 3))
                    e.matmul(psum[:, 4 + i % 4, 0:wide], xt[:, i * P:(i + 1) * P], wcat[:, :], start=True, stop=True)\
                     .then_inc(msg_ps, 1)
            e.wait_ge(consts, 2)
            e.wait_ge(frow_sb, NSEG)
            e.wait_ge(msg_act, NT)
            e.wait_ge(msg_dve, NT)
            with e.Fori(0, NSEG) as tg:
                e.wait_ge(diag_made, tg + 1)
                for v in range(2):
                    d = diag[:, v, :, :].rearrange("p a c -> p (a c)")
                    for c0, c1 in ((0, 512), (512, SW)):
                        m = e.matmul(bank2(2 * v)[:, c0:c1], ones[:, :], d[:, c0:c1], start=True, stop=True)
                m.then_inc(uv_made, 1)
                e.wait_ge(closed, tg)
                for first, lo, hi in ((True, 0, 1), (False, 1, NSEG)):
                    with ExitStack() as loop:
                        hb = 0 if first else loop.enter_context(e.Fori(lo, hi))
                        for j in range(SEG):
                            wait_weighed(e, tg * NSEG + hb, j)
                            for i in range(SEG):
                                m = e.matmul(psum[:, 4 + i // 3, i % 3 * (D + 4):i % 3 * (D + 4) + D + 1],
                                             weights[:, j, i * P:(i + 1) * P],
                                             k.msg[:, bass.ds(hb * SEG + j, 1), :].rearrange("p a f -> p (a f)"),
                                             start=first and j == 0 and i % 3 == 0, stop=j == SEG - 1,
                                             skip_group_check=True)
                            m.then_inc(summed, 1)

        @block.scalar
        def _(e):
            e.wait_ge(weights_in, 5 * 16)
            e.activation(sig[:, :], coef[:, :], ACT.Exp, scale=-1.0).then_inc(coef_exp, 1)
            with e.Fori(0, NSEG) as tb:
                e.wait_ge(xt_ps, tb + 1)
                e.wait_ge(msg_ps, tb * SEG)
                e.activation(xt, bank2(0)[:, 0:SW], ACT.Copy).then_inc(xt_sb, 1)
                e.wait_ge(frow_ps, tb + 1)
                e.activation(frow[:, bass.ts(tb, SW)].rearrange("p (s c) -> p s c", s=2), psum[:, 2:4, 0:SW // 2], ACT.Copy)\
                 .then_inc(frow_sb, 1)
                for i in range(SEG):
                    e.wait_ge(msg_ps, tb * SEG + (i + 1))
                    e.activation(k.msg[:, bass.ds(tb * SEG + i, 1), 0:D].rearrange("p a f -> p (a f)"),
                                 psum[:, 4 + i % 4, 0:D], ACT.Copy).then_inc(msg_act, 1)
            e.wait_ge(msg_dve, NT)
            for i, factor in enumerate((LEAKY, -LEAKY, 1 - LEAKY)):
                e.activation(leaky_from[:, i, :], score[:, 0, :], ACT.Copy, scale=factor).then_inc(sig_made, 1)
            e.wait_ge(sig_made, 3)
            with e.Fori(0, NSEG) as tg:
                e.wait_ge(uv_made, tg + 1)
                e.activation(leaky_to, bank2(2)[:, 0:SW], ACT.Copy).then_inc(leaky_moved, 1)
                with e.Fori(0, NSEG) as hb:
                    for j in range(SEG):
                        n = hb * SEG + j
                        total = tg * NT + n
                        p = powers[:, bass.ds(total & 3, 1), :].rearrange("p a c -> p (a c)")
                        e.wait_ge(exponents, total + 1)
                        if j in ON_POOL:
                            e.activation(p, p, ACT.Relu, bias=leaky_from[:, 1, bass.ds(n, 1)], scale=-1.0)
                            e.drain()
                            e.activation(p, p, ACT.Exp, scale=-1.0).then_inc(powered, 1)
                        else:
                            e.activation(p, p, ACT.Exp, bias=leaky_from[:, 0, bass.ds(n, 1)]).then_inc(powered, 1)
            roots(e, k, 3)

        @block.vector
        def _(e):
            e.wait_ge(wcat_ps, 1)
            e.tensor_copy(wcat[:, D:D + 2], psum[:, 0, 0:2])
            e.wait_ge(coef_exp, 1)
            e.tensor_scalar(sig[:, :], sig[:, :], 1.0, None, ALU.add)
            e.drain()
            e.tensor_copy(wfrom[:, :], wcat[:, D:D + 1].to_broadcast([P, P]))
            e.reciprocal(sig[:, :], sig[:, :])
            e.drain().then_inc(wcat_made, 1)
            with e.Fori(0, NSEG) as tb:
                e.wait_ge(xs_made, tb + 1)
                for i in range(SEG):
                    t = tb * SEG + i
                    e.wait_ge(msg_act, t + 1)
                    e.tensor_copy(score[:, :, bass.ds(t, 1)].rearrange("p a b -> p (a b)"), psum[:, 4 + i % 4, D:D + 2])
                    x = k.x[:, bass.ds(t, 1), :].rearrange("p a f -> p (a f)")
                    e.scalar_tensor_tensor(x, psum[:, 4 + i % 4, D + 2:wide], sig[:, 0:1], x, ALU.mult, ALU.add)
                    e.drain().then_inc(msg_dve, 1)
            e.wait_ge(frow_sb, NSEG)
            e.wait_ge(consts, 2)
            e.wait_ge(sig_made, 3)

            def sweep(tg, i):
                w = i % 2
                e.wait_ge(pen_in[w], (tg * (4 - w) + (i // 2 + 1)) * 16)
                e.sem_inc(dve_turn, 1)
                e.tensor_tensor_reduce(out=pen[:, w, :], in0=pen[:, w, :], in1=frow,
                                       scale=1.0, scalar=FAR, op0=ALU.add, op1=ALU.max, accum_out=best[:, i:i + 1])
                e.drain().then_inc(pen_used, 1)

            def maxima(tg):
                e.scalar_tensor_tensor(best[:, :], best[:, :], FAR / 2, best[:, :], ALU.is_gt, ALU.mult)
                e.tensor_copy(t7[:, 0, :], score[:, 1, bass.ds(tg * SEG, SEG)])
                e.drain()
                e.tensor_tensor(t7[:, 1, :], t7[:, 0, :], best[:, :], ALU.add)
                e.drain()
                e.scalar_tensor_tensor(t7[:, 1, :], t7[:, 1, :], LEAKY, t7[:, 1, :], ALU.mult, ALU.max)
                e.drain()
                e.tensor_tensor(t7[:, 2, :], t7[:, 0, :], t7[:, 1, :], ALU.subtract)
                e.scalar_tensor_tensor(t7[:, 3, :], t7[:, 0, :], LEAKY, t7[:, 1, :], ALU.mult, ALU.subtract)
                e.drain()
                for v in range(2):
                    for i in range(SEG):
                        m = e.tensor_scalar(diag[:, v, i, :], k.ident[:, :], t7[:, 2 + v, i:i + 1], None, ALU.mult)
                m.then_inc(diag_made, 1)

            def exponent(tg, b):
                n = tg * NT + b
                if b == 0:
                    e.wait_ge(leaky_moved, tg + 1)
                if b >= 4:
                    wait_weighed(e, tg * NSEG + (b - 4) // SEG, (b - 4) % SEG)
                e.scalar_tensor_tensor(powers[:, bass.ds(n & 3, 1), :].rearrange("p a c -> p (a c)"), bank2(0)[:, 0:SW],
                                       leaky_from[:, 2, b:b + 1], leaky_to, ALU.add, ALU.max)\
                 .then_inc(exponents, 1)

            def weigh(wide, tg, b):
                hb, j = divmod(b, SEG)
                if j in ON_POOL:
                    return
                n = tg * NT + b
                e.wait_ge(counts_in[hb % 2], (tg * (4 - hb % 2) + (hb // 2 + 1)) * 16)
                e.wait_ge(powered, n + 1)
                if b >= SEG:
                    e.wait_ge(summed, tg * NT + (b - SEG + 1))
                e.scalar_tensor_tensor(weights[:, j, :].rearrange("p (i c) -> p i c", c=P),
                                       powers[:, bass.ds(n & 3, 1), :].rearrange("p a (i c) -> p (a i) c", c=P), 1.0,
                                       counts[wide][hb % 2][:, :, j * P:(j + 1) * P], ALU.min, ALU.mult)\
                 .then_inc(weighed, 1)

            def blocks(wide, tg, last):
                for b in range(NT + LAG):
                    if b < NT:
                        exponent(tg, b)
                    if b >= LAG:
                        weigh(wide, tg, b - LAG)
                    if b < NT and b % SEG == SEG - 1 and not last:
                        sweep(tg + 1, b // SEG)

            def close(tg):
                e.wait_ge(summed, (tg + 1) * NT)
                for i in range(SEG):
                    e.tensor_scalar(den[:, i:i + 1], psum[:, 4 + i // 3, i % 3 * (D + 4) + D:i % 3 * (D + 4) + D + 1],
                                    1e-30, None, ALU.max)
                e.drain()
                e.reciprocal(den[:, :], den[:, :])
                e.drain()
                for i in range(SEG):
                    e.tensor_scalar(fresh[:, i, :], psum[:, 4 + i // 3, i % 3 * (D + 4):i % 3 * (D + 4) + D],
                                    den[:, i:i + 1], 0.0, ALU.mult, ALU.max)
                e.drain().then_inc(closed, 1)
                x = k.x[:, bass.ds(tg * SEG, SEG), :]
                e.tensor_tensor(x, x, fresh[:, :, :], ALU.add)
                e.drain()
                batch_stats(e, k, k.x, tg)

            def group(wide, tg, first, last):
                maxima(tg)
                if not first:
                    close(tg - 1)
                blocks(wide, tg, last)

            def program(wide):
                group(wide, 0, True, False)
                with e.Fori(1, NSEG - 1) as tg:
                    group(wide, tg, False, False)
                group(wide, NSEG - 1, False, True)
                close(NSEG - 1)

            for i in range(SEG):
                sweep(0, i)
            either(e, k, program)
            normalize(e, k, 3)


def phase_edge_sum(nc, k):
    with ExitStack() as ctx:
        sb = lambda name, shape, dt=F32: ctx.enter_context(nc.sbuf_tensor("e_" + name, shape, dt))
        sem = lambda name: ctx.enter_context(nc.semaphore("e_" + name))
        room = sb("ring", [P, NSEG, SW])
        ring = {w: [cells(room[:, i, :], w) for i in range(NSEG)] for w in (True, False)}
        parts = sb("parts", [P, NT, 2 * D], F16)
        rest = sb("rest", [P, SEG, D])
        attr = sb("attr", [P, NT, D])
        y = k.self_
        acc = ctx.enter_context(nc.psum_tensor("e_acc", [P, 2, 512], F32))
        seg_in = [sem(f"seg_in{g}") for g in range(NSEG)]
        parts_made = sem("parts_made")
        attr_in, used, taken = sem("attr_in"), sem("used"), sem("taken")
        made, stored = sem("made"), sem("stored")
        block = ctx.enter_context(nc.Block())

        @block.sync
        def _(e):
            e.dma_start(attr[:, :, :].rearrange("p t f -> p (t f)"), k.attr_d).then_inc(attr_in, 16)

            def program(wide):
                with e.Fori(0, NT) as t:
                    for g in range(NSEG):
                        e.wait_ge(used, t * NSEG + (g + 1))
                        e.dma_start(ring[wide][g], k.cs_d[wide][bass.ds(t, 1), :, g * SW:(g + 1) * SW]
                                    .rearrange("a p c -> (a p) c")).then_inc(seg_in[g], 16)

            either(e, k, program)
            e.wait_ge(made, 1)
            full = NT - 1
            e.dma_start(k.out[0:full * P, :].rearrange("(t p) f -> p t f", p=P), y[:, 0:full, :]).then_inc(stored, 16)
            e.dma_start(k.out[full * P:NODES, :], y[0:LAST, full, :]).then_inc(stored, 16)
            e.wait_ge(stored, 32)

        @block.tensor
        def _(e):
            e.sem_inc(used, NSEG)

            def program(wide):
                n = D if wide else 2 * D
                with e.Fori(0, NT) as t:
                    e.wait_ge(taken, t + 1)
                    for g in range(NSEG):
                        e.wait_ge(seg_in[g], (t + 1) * 16)
                        e.wait_ge(parts_made, g + 1)
                        for i in range(SEG):
                            x = k.x[:, g * SEG + i, :] if wide else parts[:, g * SEG + i, :]
                            m = e.matmul(acc[:, bass.ds(t & 1, 1), 0:n].rearrange("p a f -> p (a f)"),
                                         ring[wide][g][:, i * P:(i + 1) * P], x,
                                         start=g == 0 and i == 0, stop=g == NSEG - 1 and i == SEG - 1)
                        m.then_inc(used, 1)

            either(e, k, program)

        @block.scalar
        def _(e):
            roots(e, k, 4)

        @block.vector
        def _(e):
            e.sem_inc(taken, 2)
            with e.Fori(0, NSEG) as tb:
                split_rows(e, k.x, parts, rest[:, :, :], tb, parts_made)
            e.wait_ge(attr_in, 16)

            def program(wide):
                with e.Fori(0, NT) as t:
                    row = lambda a: a[:, bass.ds(t, 1), :].rearrange("p a f -> p (a f)")
                    e.tensor_tensor(row(y), row(k.x), row(attr), ALU.add)
                    e.drain()
                    e.wait_ge(used, t * NSEG + 2 * NSEG)
                    for q in range(1 if wide else 2):
                        e.scalar_tensor_tensor(row(y), acc[:, bass.ds(t & 1, 1), q * D:(q + 1) * D]
                                               .rearrange("p a f -> p (a f)"), 1.0 if wide else 1 / SCALE, row(y),
                                               ALU.mult, ALU.add)
                        m = e.drain()
                    m.then_inc(taken, 1)
                    tile_stats(e, k, row(y), t)

            either(e, k, program)
            normalize(e, k, 4, made, y)


def layout(inputs):
    import numpy as np

    a = {n: np.asarray(v) for n, v in inputs.items()}
    edges = EPAD - EDGES
    got = {n: v for n, v in a.items() if n.startswith("L0")}
    got["x"] = np.pad(a["x"], ((0, NPAD - NODES), (0, 0)))
    got["x_transposed"] = np.ascontiguousarray(got["x"].T)
    got["src"] = np.pad(a["src"], (0, edges))
    got["dst"] = np.pad(a["dst"], (0, edges), constant_values=PAD_DST)
    got["edge_type_8"] = np.pad(a["edge_type_8"], (0, edges))
    got["edge_attr_128"] = np.pad(a["edge_attr_128"], ((0, edges), (0, 0)))
    got["w_msg"] = a["L2_gnn_W_msg"]
    got["w_msg_transposed"] = np.ascontiguousarray(a["L2_gnn_W_msg"].T)
    got["w_res_transposed"] = np.ascontiguousarray(a["L2_gnn_W_res"].T)
    got["attn_w"] = a["L2_gnn_attn_w"]
    got["coef"] = a["L2_gnn_passthrough_coef"]
    return got


def kernel(**inputs):
    import numpy as np
    import concourse.bacc as bacc
    from concourse.bass_utils import run_bass_kernel_spmd

    nc = bacc.Bacc("TRN2", target_bir_lowering=False, num_devices=1)
    arrays = {f"in_{n}": v for n, v in layout(inputs).items()}
    ins = {n[3:]: nc.dram_tensor(n, v.shape, mybir.dt.from_np(v.dtype), kind="ExternalInput").ap()
           for n, v in arrays.items()}
    out = nc.dram_tensor("out", (NODES, D), F32, kind="ExternalOutput").ap()
    build(nc, ins, out)
    return run_bass_kernel_spmd(nc, [arrays], core_ids=[0]).results[0]["out"]
```
